# Optimizing a Trainium2 kernel written in Bass

```python
import numpy as np
import jax
import jax.numpy as jnp

def _softmax(x, axis=-1):
    return jax.nn.softmax(x, axis=axis)

def _gelu(x):
    return jax.nn.gelu(x, approximate=True)

def _silu(x):
    return jax.nn.silu(x)

def _sigmoid(x):
    return jax.nn.sigmoid(x)

def _layernorm(x, axis=-1, eps=1e-05):
    m = jnp.mean(x, axis=axis, keepdims=True)
    v = jnp.var(x, axis=axis, keepdims=True)
    return (x - m) / jnp.sqrt(v + eps)

def _scatter_add(tgt, idx, src, axis=0):
    return tgt.at[idx].add(src)

def _segment_sum(src, seg, n):
    return jax.ops.segment_sum(src, seg, n)
kernel_name = 'mk_adaln_ffn_d2_seqx_r8_21e392'

def setup_inputs(seed: int=0):
    np.random.seed(seed)
    _w = jnp.asarray

    def _rec_inputs():
        import jax
        import jax.numpy as jnp
        _rk = jax.random.key(seed)
        x = -0.000125 + 0.9999 * jax.random.normal(jax.random.fold_in(_rk, 1), (128, 32, 512), jnp.float32)
        _lenS = 32 - jax.random.randint(jax.random.fold_in(_rk, 7), (128,), 0, max(1, 32 // 4) + 1, jnp.int32)
        _lenS2 = 32 - jax.random.randint(jax.random.fold_in(_rk, 8), (128,), 0, max(1, 32 // 4) + 1, jnp.int32)
        cond_128 = 0.0061147 + 1.02565 * jax.random.normal(jax.random.fold_in(_rk, 11), (128, 128), jnp.float32)
        fside_S_0 = -0.022604 + 0.987366 * jax.random.normal(jax.random.fold_in(_rk, 12), (32,), jnp.float32)
        return (x, cond_128, fside_S_0)
    x, cond_128, fside_S_0 = _rec_inputs()

    def _L0_cond_setup():
        import jax, jax.numpy as jnp
        import numpy as np
        from jax import lax
        N, C_IN, L = (32, 32, 512)
        C_OUT, K, GROUPS = (32, 9, 4)
        C_DIM, PAD, STRIDE = (128, 4, 1)
        key = jax.random.key(seed)
        k1, k2, k3, k4, k5 = jax.random.split(key, 5)
        x = jax.random.normal(k1, (N, C_IN, L), dtype=jnp.float32)
        c = jax.random.normal(k2, (N, C_DIM), dtype=jnp.float32)
        weight = jax.random.normal(k3, (C_OUT, C_IN // GROUPS, K), dtype=jnp.float32)
        c_weight = jax.random.normal(k4, (C_OUT, C_DIM), dtype=jnp.float32)
        bias = jax.random.normal(k5, (C_OUT,), dtype=jnp.float32)
        return {'x': x, 'c': c, 'weight': weight, 'c_weight': c_weight, 'bias': bias}
    _L0_cond_all = _L0_cond_setup()
    _L0_cond_in = {k: v for k, v in _L0_cond_all.items() if k in ('weight', 'c_weight')}
    del _L0_cond_all

    def _L0_ffn_setup():
        import jax, jax.numpy as jnp
        import numpy as np
        NUM_EXPERTS = 8
        TOP_K = 2
        RANK = 16
        LORA_ALPHA = 32
        SCALING = LORA_ALPHA / RANK
        key = jax.random.key(seed)
        ks = jax.random.split(key, 6)
        B, S, D_IN, D_OUT = (4, 256, 512, 512)
        x = jax.random.normal(ks[0], (B, S, D_IN), dtype=jnp.float32)
        W_base = jax.random.normal(ks[1], (D_OUT, D_IN), dtype=jnp.float32) * 0.02
        b_base = jax.random.normal(ks[2], (D_OUT,), dtype=jnp.float32) * 0.02
        W_router = jax.random.normal(ks[3], (NUM_EXPERTS, D_IN), dtype=jnp.float32) * 0.02
        A = jax.random.normal(ks[4], (NUM_EXPERTS, RANK, D_IN), dtype=jnp.float32) * 0.02
        Bm = jax.random.normal(ks[5], (D_OUT, RANK), dtype=jnp.float32) * 0.02
        Bm = jnp.broadcast_to(Bm, (NUM_EXPERTS, D_OUT, RANK)) * jnp.arange(1, NUM_EXPERTS + 1, dtype=jnp.float32)[:, None, None] * 0.2
        return {'x': x, 'W_base': W_base, 'b_base': b_base, 'W_router': W_router, 'A': A, 'B': Bm}
    _L0_ffn_all = _L0_ffn_setup()
    _L0_ffn_in = {k: v for k, v in _L0_ffn_all.items() if k in ('W_base', 'b_base', 'W_router', 'A', 'B')}
    del _L0_ffn_all

    def _L1_cond_setup():
        import jax, jax.numpy as jnp
        import numpy as np
        K = 8
        T = 1.0
        D_EMBD = 128
        IN_C = 32
        OUT_C = 32
        BS = 32
        H = 512
        HID = 128
        key = jax.random.key(seed)
        ks = jax.random.split(key, 10)
        s = lambda fan_in: 1.0 / np.sqrt(fan_in)
        return {'x': jax.random.normal(ks[0], (BS, IN_C, H), dtype=jnp.float32), 'embedding': jax.random.normal(ks[1], (BS, D_EMBD), dtype=jnp.float32), 'W0': jax.random.normal(ks[2], (D_EMBD, HID), dtype=jnp.float32) * s(D_EMBD), 'b0': jnp.zeros((HID,), dtype=jnp.float32), 'W1': jax.random.normal(ks[3], (HID, HID), dtype=jnp.float32) * s(HID), 'b1': jnp.zeros((HID,), dtype=jnp.float32), 'W2': jax.random.normal(ks[4], (HID, K), dtype=jnp.float32) * s(HID), 'b2': jnp.zeros((K,), dtype=jnp.float32), 'weight': jax.random.normal(ks[5], (K, OUT_C, IN_C, 1), dtype=jnp.float32) * s(IN_C), 'bias_k': jax.random.normal(ks[6], (K, OUT_C), dtype=jnp.float32) * 0.1}
    _L1_cond_all = _L1_cond_setup()
    _L1_cond_in = {k: v for k, v in _L1_cond_all.items() if k in ('W0', 'b0', 'W1', 'b1', 'W2', 'b2', 'weight', 'bias_k')}
    del _L1_cond_all

    def _L1_ffn_setup():
        import jax, jax.numpy as jnp
        import numpy as np
        R = 16
        NUM_EXPERTS = 8
        TOP_K = 2
        LORA_ALPHA = 32
        SCALING = LORA_ALPHA / R
        key = jax.random.key(seed)
        ks = jax.random.split(key, 6)
        d_in, d_out = (512, 512)
        x = jax.random.normal(ks[0], (4, 256, d_in), dtype=jnp.float32)
        W_base = jax.random.normal(ks[1], (d_out, d_in), dtype=jnp.float32) * 0.02
        b_base = jax.random.normal(ks[2], (d_out,), dtype=jnp.float32) * 0.02
        W_router = jax.random.normal(ks[3], (NUM_EXPERTS, d_in), dtype=jnp.float32) * 0.01
        A = jax.random.normal(ks[4], (NUM_EXPERTS, R, d_in), dtype=jnp.float32) * 0.02
        B = jax.random.normal(ks[5], (NUM_EXPERTS, d_out, R), dtype=jnp.float32) * 0.02
        return {'x': x, 'W_base': W_base, 'b_base': b_base, 'W_router': W_router, 'A': A, 'B': B}
    _L1_ffn_all = _L1_ffn_setup()
    _L1_ffn_in = {k: v for k, v in _L1_ffn_all.items() if k in ('W_base', 'b_base', 'W_router', 'A', 'B')}
    del _L1_ffn_all
    return {'x': x, 'cond_128': cond_128, 'fside_S_0': fside_S_0, 'L0_cond_weight': _L0_cond_in['weight'], 'L0_cond_c_weight': _L0_cond_in['c_weight'], 'L0_ffn_W_base': _L0_ffn_in['W_base'], 'L0_ffn_b_base': _L0_ffn_in['b_base'], 'L0_ffn_W_router': _L0_ffn_in['W_router'], 'L0_ffn_A': _L0_ffn_in['A'], 'L0_ffn_B': _L0_ffn_in['B'], 'L1_cond_W0': _L1_cond_in['W0'], 'L1_cond_b0': _L1_cond_in['b0'], 'L1_cond_W1': _L1_cond_in['W1'], 'L1_cond_b1': _L1_cond_in['b1'], 'L1_cond_W2': _L1_cond_in['W2'], 'L1_cond_b2': _L1_cond_in['b2'], 'L1_cond_weight': _L1_cond_in['weight'], 'L1_cond_bias_k': _L1_cond_in['bias_k'], 'L1_ffn_W_base': _L1_ffn_in['W_base'], 'L1_ffn_b_base': _L1_ffn_in['b_base'], 'L1_ffn_W_router': _L1_ffn_in['W_router'], 'L1_ffn_A': _L1_ffn_in['A'], 'L1_ffn_B': _L1_ffn_in['B']}

def reference(x, cond_128, fside_S_0, L0_cond_weight, L0_cond_c_weight, L0_ffn_W_base, L0_ffn_b_base, L0_ffn_W_router, L0_ffn_A, L0_ffn_B, L1_cond_W0, L1_cond_b0, L1_cond_W1, L1_cond_b1, L1_cond_W2, L1_cond_b2, L1_cond_weight, L1_cond_bias_k, L1_ffn_W_base, L1_ffn_b_base, L1_ffn_W_router, L1_ffn_A, L1_ffn_B):
    import jax
    import jax.numpy as jnp

    def _L0_cond_ref(x, c, weight, c_weight, bias):
        import jax, jax.numpy as jnp
        import numpy as np
        from jax import lax
        N, C_IN, L = (32, 32, 512)
        C_OUT, K, GROUPS = (32, 9, 4)
        C_DIM, PAD, STRIDE = (128, 4, 1)
        out = lax.conv_general_dilated(x, weight, window_strides=(STRIDE,), padding=[(PAD, PAD)], dimension_numbers=('NCH', 'OIH', 'NCH'), feature_group_count=GROUPS)
        ctx = jnp.einsum('nd,od->no', c, c_weight)
        out = out + ctx[:, :, None] + bias[None, :, None]
        return out

    def _L0_ffn_ref(x, W_base, b_base, W_router, A, B):
        import jax, jax.numpy as jnp
        import numpy as np
        NUM_EXPERTS = 8
        TOP_K = 2
        RANK = 16
        LORA_ALPHA = 32
        SCALING = LORA_ALPHA / RANK
        bs, seq, d_in = x.shape
        T = bs * seq
        xf = x.reshape(T, d_in)
        base = xf @ W_base.T + b_base
        logits = xf @ W_router.T
        rw, sel = jax.lax.top_k(logits, TOP_K)
        rw = jax.nn.softmax(rw, axis=-1)
        onehot = jax.nn.one_hot(sel, NUM_EXPERTS, dtype=rw.dtype)
        w = jnp.einsum('tk,tke->te', rw, onehot)
        h = jnp.einsum('td,erd->ter', xf, A)
        lora = jnp.einsum('ter,te,eor->to', h, w, B) * SCALING
        return (base + lora).reshape(bs, seq, -1)

    def _L1_cond_ref(x, embedding, W0, b0, W1, b1, W2, b2, weight, bias_k):
        import jax, jax.numpy as jnp
        import numpy as np
        K = 8
        T = 1.0
        D_EMBD = 128
        IN_C = 32
        OUT_C = 32
        BS = 32
        H = 512
        HID = 128
        h = jax.nn.gelu(embedding @ W0 + b0, approximate=False)
        h = jax.nn.gelu(h @ W1 + b1, approximate=False)
        att = jax.nn.softmax((h @ W2 + b2) / T, axis=-1)
        agg_w = jnp.einsum('bk,koi->boi', att, weight[..., 0])
        agg_b = att @ bias_k
        out = jnp.einsum('boi,bih->boh', agg_w, x) + agg_b[:, :, None]
        return out

    def _L1_ffn_ref(x, W_base, b_base, W_router, A, B):
        import jax, jax.numpy as jnp
        import numpy as np
        R = 16
        NUM_EXPERTS = 8
        TOP_K = 2
        LORA_ALPHA = 32
        SCALING = LORA_ALPHA / R
        orig_shape = x.shape
        d_in = x.shape[-1]
        x_flat = x.reshape(-1, d_in)
        logits = x_flat @ W_router.T
        probs = jax.nn.softmax(logits, axis=-1)
        topk_probs, topk_idx = jax.lax.top_k(probs, TOP_K)
        topk_probs = topk_probs / jnp.sum(topk_probs, axis=-1, keepdims=True)
        onehot = jax.nn.one_hot(topk_idx, NUM_EXPERTS, dtype=x.dtype)
        combine = jnp.einsum('nk,nke->ne', topk_probs, onehot)
        h = jnp.einsum('nd,erd->ner', x_flat, A)
        hw = h * combine[:, :, None]
        expert_out = jnp.einsum('ner,eor->no', hw, B) * SCALING
        base_out = x_flat @ W_base.T + b_base
        out = base_out + expert_out
        return out.reshape(*orig_shape[:-1], W_base.shape[0])
    x = x + _L0_ffn_ref(_L0_cond_ref(x, cond_128, L0_cond_weight, L0_cond_c_weight, fside_S_0), L0_ffn_W_base, L0_ffn_b_base, L0_ffn_W_router, L0_ffn_A, L0_ffn_B)
    x = x + _L1_ffn_ref(_L1_cond_ref(x, cond_128, L1_cond_W0, L1_cond_b0, L1_cond_W1, L1_cond_b1, L1_cond_W2, L1_cond_b2, L1_cond_weight, L1_cond_bias_k), L1_ffn_W_base, L1_ffn_b_base, L1_ffn_W_router, L1_ffn_A, L1_ffn_B)
    return x

_drawn_inputs = setup_inputs


def setup_inputs(seed=0):
    import zlib

    import numpy as np

    out = dict(_drawn_inputs(seed))
    spreads = {'L1_cond_b0': (0.0, 0.8), 'L1_cond_b1': (0.0, 0.795), 'L1_cond_b2': (0.0, 0.635)}
    factors = {'L0_ffn_b_base': 8.0,
     'L1_cond_bias_k': 8.0,
     'L1_ffn_b_base': 8.0,
     'L1_ffn_W_router': 3.542,
     'L1_ffn_A': 3.061,
     'L1_ffn_B': 2.983}
    for name, (base, spread) in spreads.items():
        noise = np.random.default_rng([zlib.crc32(name.encode()), seed]).standard_normal(out[name].shape)
        drawn = base * np.exp(spread * noise) if base else spread * noise
        out[name] = jnp.asarray(drawn.astype(out[name].dtype))
    for name, factor in factors.items():
        out[name] = (out[name] * factor).astype(out[name].dtype)
    return out
```

```python
import concourse.bass as bass
from concourse import mybir
from contextlib import ExitStack

F32 = mybir.dt.float32
F32R = mybir.dt.float32r
U32 = mybir.dt.uint32
ALU = mybir.AluOpType
ACT = mybir.ActivationFunctionType
AX = mybir.AxisListType

P = 128
N, C, D = 128, 32, 512
SPT = P // C
TILES = N // SPT
TAPS, GROUPS = 9, 4
PH = 4
NB = D // PH
NBP = NB + 2
SHIFTS = 3
KT = D // P
E, R = 8, 16
ER = E * R
AR = ER + E
SCALING = 2.0
HI, LO = 0, 1
SPLITS = [(HI, HI), (HI, LO), (LO, HI)]
LINKS = 9


def build(nc, d):
    ctx = ExitStack()
    with ctx:
        def sb(name, shape, dt=F32):
            return ctx.enter_context(nc.sbuf_tensor(name, shape, dt))

        def bank(name):
            return ctx.enter_context(nc.psum_tensor(name, [P, 512], F32))

        def sem(name):
            return ctx.enter_context(nc.semaphore(name))

        conv_raw = sb("conv_raw", [P, SHIFTS, P])
        conv_w = sb("conv_w", [P, 2, SHIFTS, P], F32R)
        base_raw = sb("base_raw", [P, KT, D])
        ar_raw = [sb(f"ar_raw{y}", [P, KT, AR]) for y in range(2)]
        lb_raw = [sb(f"lb_raw{y}", [P, D]) for y in range(2)]
        base_raw1 = sb("base_raw1", [P, KT, D])
        base_raws = [base_raw, base_raw1]
        base_w = [sb(f"base_w{y}", [P, 2, KT, D], F32R) for y in range(2)]
        ar_w = [sb(f"ar_w{y}", [P, KT, 2, AR], F32R) for y in range(2)]
        lb_w = [sb(f"lb_w{y}", [P, 2, D], F32R) for y in range(2)]
        bias = [sb(f"bias{y}", [P, D]) for y in range(2)]
        ident = sb("ident", [P, P])
        iota = sb("iota", [P, E])
        condT = sb("condT", [P, N])
        cw_sb = sb("cw_sb", [P, P])
        side_sb = sb("side_sb", [P, 1])
        conv_bias = sb("conv_bias", [P, N])
        w01 = sb("w01", [P, 2, P])
        w2_sb = sb("w2_sb", [P, E])
        b01 = sb("b01", [P, 2])
        b2_sb = sb("b2_sb", [P, E])
        hid = sb("hid", [P, 2, N])
        att = sb("att", [P, 4, E])
        att_s = sb("att_s", [P, 4])
        own = sb("own", [P, SPT, E])
        att_m = sb("att_m", [P, SPT, E])
        att_mT = sb("att_mT", [SPT * E, N])
        kern_sb = sb("kern_sb", [SPT * E, C, P])
        bk_sb = sb("bk_sb", [SPT * E, P])
        mix = sb("mix", [P, N, C])
        mix_bias = sb("mix_bias", [P, TILES])
        x_raw = sb("x_raw", [P, SPT, NBP])
        x_part = [sb(f"x_part{p}", [P, SPT, NBP], F32R) for p in range(2)]
        x_tok = sb("x_tok", [P, D])
        xb = sb("xb", [P, D])
        y0 = sb("y0", [P, SPT, NB])
        x1 = sb("x1", [P, D])
        x1b = sb("x1b", [P, D])
        x1_part = [sb(f"x1_part{p}", [P, D], F32R) for p in range(2)]
        mix_part = [sb(f"mix_part{p}", [P, P], F32R) for p in range(2)]
        y1 = sb("y1", [P, D])
        yT = [[sb(f"yT{y}_{p}", [P, KT, P], F32R) for p in range(2)] for y in range(2)]
        res = sb("res", [P, D])
        ar_lo = [sb(f"ar_lo{y}", [P, AR]) for y in range(2)]
        ar = [sb(f"ar{y}", [P, AR]) for y in range(2)]
        top = [sb(f"top{y}", [P, 8]) for y in range(2)]
        top_i = [sb(f"top_i{y}", [P, 8], U32) for y in range(2)]
        top_f = [sb(f"top_f{y}", [P, 2]) for y in range(2)]
        ratio = [sb(f"ratio{y}", [P, 1]) for y in range(2)]
        denom = [sb(f"denom{y}", [P, 1]) for y in range(2)]
        wts = [sb(f"wts{y}", [P, 2]) for y in range(2)]
        gates = [sb(f"gates{y}", [P, 3, E]) for y in range(2)]
        hw = [sb(f"hw{y}", [P, ER]) for y in range(2)]
        hwT = [[sb(f"hwT{y}_{p}", [P, P], F32R) for p in range(2)] for y in range(2)]

        ps_conv, ps_t0, ps_mix, ps_t1 = bank("ps_conv"), bank("ps_t0"), bank("ps_mix"), bank("ps_t1")
        ps_out = [bank("ps_out0"), bank("ps_out1")]
        ps_ar = [bank("ps_ar0"), bank("ps_ar1")]
        HWT = slice(2 * AR, 2 * AR + P)

        l_conv, l_base, l_ar, l_lb, l_bias = sem("l_conv"), [sem("l_base0"), sem("l_base1")], \
            [sem("l_ar0"), sem("l_ar1")], [sem("l_lb0"), sem("l_lb1")], [sem("l_bias0"), sem("l_bias1")]
        l_const, l_cond, l_mlp, l_kern = sem("l_const"), sem("l_cond"), sem("l_mlp"), sem("l_kern")
        x_loaded, tok_loaded, stored = sem("x_loaded"), sem("tok_loaded"), sem("stored")
        conv_w_hi, conv_w_lo = sem("conv_w_hi"), sem("conv_w_lo")
        w_hi = [sem("w_hi0"), sem("w_hi1")]
        w_lo = [sem("w_lo0"), sem("w_lo1")]
        cb_mm, cb_ready = sem("cb_mm"), sem("cb_ready")
        mlp_mm, mlp_act, mlp_dve = sem("mlp_mm"), sem("mlp_act"), sem("mlp_dve")
        mixk_mm, mixk_ready, mixb_ready = sem("mixk_mm"), sem("mixk_ready"), sem("mixb_ready")
        names = ["xh", "xl", "xb", "conv", "y0", "t0", "x1", "x1h", "x1l", "x1b", "mh", "ml",
                 "mix", "y1", "t1", "out"]
        s = {n: sem("s_" + n) for n in names}
        for n in ["ar", "arlo", "top", "ratio", "hw", "hwt", "hwh", "hwl", "yh", "yl", "b", "route"]:
            s[n] = [sem(f"s_{n}{y}") for y in range(2)]

        def need(eng, semaphore, value):
            if isinstance(value, int) and value <= 0:
                return
            eng.wait_ge(semaphore, value)

        def stages(eng, step):
            def at(t):
                step(t, lambda k: 0 <= t + k < TILES)
            for t in range(-1, 3):
                at(t)
            with eng.Fori(3, TILES - 2) as t:
                step(t, lambda k: True)
            for t in range(TILES - 2, TILES + 2):
                at(t)

        block = ctx.enter_context(nc.Block())

        @block.sync
        def _(sp):
            def load_x(t):
                need(sp, s["xh"], t)
                need(sp, s["xl"], t)
                sp.dma_start(x_raw[:, :, :], d["x_phase"][t]).then_inc(x_loaded, 16)

            def load_tok(t):
                need(sp, s["xb"], t)
                sp.dma_start(x_tok[:, :], d["x_tok"][t]).then_inc(tok_loaded, 16)

            sp.dma_start(conv_raw[:, :, :], d["conv_w"]).then_inc(l_conv, 16)
            load_x(0)
            sp.dma_start(ar_raw[0][:, :, :], d["ar0"]).then_inc(l_ar[0], 16)
            sp.dma_start(base_raws[0][:, :, :], d["base0"]).then_inc(l_base[0], 16)
            sp.dma_start(lb_raw[0][:, :], d["lb0"]).then_inc(l_lb[0], 16)
            sp.dma_start(bias[0][:, :], d["bias0"]).then_inc(l_bias[0], 16)
            load_tok(0)
            load_x(1)
            sp.dma_start(kern_sb[:, :, :], d["kern"]).then_inc(l_kern, 16)
            sp.dma_start(bk_sb[:, :], d["bk"]).then_inc(l_kern, 16)
            sp.dma_start(ar_raw[1][:, :, :], d["ar1"]).then_inc(l_ar[1], 16)
            sp.dma_start(base_raws[1][:, :, :], d["base1"]).then_inc(l_base[1], 16)
            sp.dma_start(lb_raw[1][:, :], d["lb1"]).then_inc(l_lb[1], 16)
            sp.dma_start(bias[1][:, :], d["bias1"]).then_inc(l_bias[1], 16)

            def step(t, has):
                if has(0) and has(1):
                    load_tok(t + 1)
                if has(0) and has(2):
                    load_x(t + 2)
                if has(-2):
                    sp.wait_ge(s["out"], t - 1)
                    sp.dma_start(d["out"][t - 2], res[:, :]).then_inc(stored, 16)
            stages(sp, step)
            sp.wait_ge(stored, 16 * TILES)

        @block.tensor
        def _(pe):
            mm = nc.tensor.matmul

            def conv(t):
                if isinstance(t, int) and t == 0:
                    pe.wait_ge(conv_w_hi, 1)
                    pe.wait_ge(conv_w_lo, 1)
                need(pe, s["y0"], t)
                pe.wait_ge(s["xh"], t + 1)
                pairs = [(shift, dp, wp) for dp, wp in SPLITS for shift in range(SHIFTS)]
                for n, (shift, dp, wp) in enumerate(pairs):
                    if n == 2 * SHIFTS:
                        pe.wait_ge(s["xl"], t + 1)
                    last = mm(ps_conv[:, :], conv_w[:, wp, shift, :], x_part[dp][:, :, shift:shift + NB],
                              start=(n == 0), stop=(n == len(pairs) - 1))
                last.then_inc(s["conv"], 1)

            def turn(y, src, dst, ready, free, done, t):
                need(pe, free, t)
                pe.wait_ge(ready, t + 1)
                for k in range(KT):
                    last = nc.tensor.transpose(dst[:, k * P:(k + 1) * P], src[:, k * P:(k + 1) * P], ident[:, :])
                last.then_inc(done, 1)

            def ar_product(y, t):
                if isinstance(t, int) and t == 0:
                    pe.wait_ge(w_hi[y], 1)
                    pe.wait_ge(w_lo[y], 1)
                need(pe, s["hwl"][y], t)
                pe.wait_ge(s["yh"][y], t + 1)
                for k in range(KT):
                    mm(ps_ar[y][:, 0:2 * AR], yT[y][HI][:, k, :],
                       ar_w[y][:, k, :, :].rearrange("p a b -> p (a b)"), start=(k == 0), stop=False,
                       skip_group_check=True)
                pe.wait_ge(s["yl"][y], t + 1)
                for k in range(KT):
                    last = mm(ps_ar[y][:, 0:AR], yT[y][LO][:, k, :], ar_w[y][:, k, HI, :],
                              start=False, stop=(k == KT - 1), skip_group_check=True)
                last.then_inc(s["ar"][y], 1)

            def base_product(y, t, half):
                if half == 0:
                    if isinstance(t, int) and t == 0:
                        pe.wait_ge(w_hi[y], 2)
                        pe.wait_ge(w_lo[y], 2)
                    need(pe, s["x1"] if y == 0 else s["out"], t)
                for k in range(half * KT // 2, (half + 1) * KT // 2):
                    for n, (dp, wp) in enumerate(SPLITS):
                        mm(ps_out[y][:, :], yT[y][dp][:, k, :], base_w[y][:, wp, k, :],
                           start=(k == 0 and n == 0), stop=False)

            def turn_hw(y, t):
                pe.wait_ge(s["hw"][y], t + 1)
                nc.tensor.transpose(ps_ar[y][:, HWT], hw[y][:, :], ident[:, :]).then_inc(s["hwt"][y], 1)

            def b_product(y, t):
                if isinstance(t, int) and t == 0:
                    pe.wait_ge(w_hi[y], 3)
                    pe.wait_ge(w_lo[y], 3)
                pe.wait_ge(s["hwh"][y], t + 1)
                for n, (dp, wp) in enumerate(SPLITS):
                    if dp == LO:
                        pe.wait_ge(s["hwl"][y], t + 1)
                    last = mm(ps_out[y][:, :], hwT[y][dp][:, :], lb_w[y][:, wp, :],
                              start=False, stop=(n == len(SPLITS) - 1))
                last.then_inc(s["b"][y], 1)

            def mix_product(t):
                need(pe, s["y1"], t)
                for p, q in ((s["x1h"], s["mh"]), (s["x1l"], s["ml"])):
                    pe.wait_ge(p, t + 1)
                    pe.wait_ge(q, t + 1)
                for n, (dp, wp) in enumerate(SPLITS):
                    last = mm(ps_mix[:, :], mix_part[wp][:, :], x1_part[dp][:, :],
                              start=(n == 0), stop=(n == len(SPLITS) - 1))
                last.then_inc(s["mix"], 1)

            pe.wait_ge(l_cond, 48)
            mm(ps_mix[:, 0:N], cw_sb[:, :], condT[:, :], start=True, stop=True).then_inc(cb_mm, 1)
            pe.wait_ge(l_mlp, 96)
            mm(ps_t1[:, 0:N], w01[:, 0, :], condT[:, :], start=True, stop=True).then_inc(mlp_mm, 1)
            pe.wait_ge(mlp_act, 1)
            mm(ps_t1[:, N:2 * N], w01[:, 1, :], hid[:, 0, :], start=True, stop=True).then_inc(mlp_mm, 1)
            pe.wait_ge(mlp_act, 2)
            mm(ps_t1[:, 2 * N:2 * N + E], hid[:, 1, :], w2_sb[:, :], start=True, stop=True).then_inc(mlp_mm, 1)

            def mixing_setup():
                pe.wait_ge(mlp_dve, 4)
                nc.tensor.transpose(ps_t1[0:SPT * E, 0:N], att_m[:, :, :].rearrange("p a b -> p (a b)"),
                                    ident[:, :]).then_inc(mlp_mm, 1)
                pe.wait_ge(mlp_dve, 5)
                pe.wait_ge(l_kern, 32)
                mm(ps_t1[:, N:2 * N], bk_sb[:, :], att_mT[:, :], start=True, stop=True).then_inc(mlp_mm, 1)
                for q in range(C // 4):
                    if q >= 2:
                        pe.wait_ge(mixk_ready, q - 1)
                    ps = (ps_mix, ps_out[1])[q % 2]
                    for c in range(4):
                        last = mm(ps[:, c * N:(c + 1) * N], kern_sb[:, 4 * q + c, :], att_mT[:, :],
                                  start=True, stop=True)
                    last.then_inc(mixk_mm, 1)

            def step(t, has):
                if has(0):
                    ar_product(0, t)
                if has(-2):
                    b_product(1, t - 2)
                if has(-1):
                    mix_product(t - 1)
                if has(0):
                    base_product(0, t, 0)
                if has(-1):
                    turn(1, y1, ps_t1, s["y1"], s["yl"][1], s["t1"], t - 1)
                if has(0):
                    base_product(0, t, 1)
                    turn_hw(0, t)
                if has(-1):
                    ar_product(1, t - 1)
                if has(0):
                    b_product(0, t)
                if isinstance(t, int) and t == 0:
                    mixing_setup()
                if has(1):
                    conv(t + 1)
                if has(-1):
                    base_product(1, t - 1, 0)
                if has(1):
                    if isinstance(t, int) and t == -1:
                        pe.wait_ge(l_const, 48)
                    turn(0, y0[:, :, :].rearrange("p a b -> p (a b)"), ps_t0, s["y0"], s["yl"][0],
                         s["t0"], t + 1)
                if has(-1):
                    base_product(1, t - 1, 1)
                    turn_hw(1, t - 1)
            stages(pe, step)

        @block.scalar
        def _(act):
            def copy(dst, src):
                return nc.scalar.activation(dst, src, ACT.Copy)

            act.dma_start(condT[:, :], d["condT"]).then_inc(l_cond, 16)
            act.dma_start(cw_sb[:, :], d["cw"]).then_inc(l_cond, 16)
            act.dma_start(side_sb[:, :], d["side"]).then_inc(l_cond, 16)
            act.dma_start(w01[:, 0, :], d["W0"]).then_inc(l_mlp, 16)
            act.dma_start(w01[:, 1, :], d["W1"]).then_inc(l_mlp, 16)
            act.dma_start(w2_sb[:, :], d["W2"]).then_inc(l_mlp, 16)
            act.dma_start(b01[:, 0:1], d["b0"]).then_inc(l_mlp, 16)
            act.dma_start(b01[:, 1:2], d["b1"]).then_inc(l_mlp, 16)
            act.dma_start(b2_sb[:, :], d["b2"]).then_inc(l_mlp, 16)
            act.dma_start(ident[:, :], d["ident"]).then_inc(l_const, 16)
            act.dma_start(iota[:, :], d["iota"]).then_inc(l_const, 16)
            act.dma_start(own[:, :, :], d["own"]).then_inc(l_const, 16)

            def split_x(t):
                act.wait_ge(x_loaded, 16 * (t + 1))
                need(act, s["conv"], t)
                copy(x_part[HI][:, :, :], x_raw[:, :, :]).then_inc(s["xh"], 1)

            def split_weights(y):
                act.wait_ge(l_ar[y], 16)
                copy(ar_w[y][:, :, HI, :], ar_raw[y][:, :, :]).then_inc(w_hi[y], 1)
                act.wait_ge(l_base[y], 16)
                copy(base_w[y][:, HI, :, :], base_raws[y][:, :, :]).then_inc(w_hi[y], 1)
                act.wait_ge(l_lb[y], 16)
                copy(lb_w[y][:, HI, :], lb_raw[y][:, :]).then_inc(w_hi[y], 1)

            act.wait_ge(l_conv, 16)
            copy(conv_w[:, HI, :, :], conv_raw[:, :, :]).then_inc(conv_w_hi, 1)
            split_x(0)
            for n in range(2):
                act.wait_ge(mlp_mm, n + 1)
                nc.scalar.activation(hid[:, n, :], ps_t1[:, n * N:(n + 1) * N], ACT.Gelu,
                                     bias=b01[:, n:n + 1]).then_inc(mlp_act, 1)
            split_weights(0)
            act.wait_ge(mlp_dve, 2)
            nc.scalar.activation(att[:, 1, :], att[:, 0, :], ACT.Exp, bias=att_s[:, 0:1],
                                 accum_out=att_s[:, 1:2]).then_inc(mlp_act, 1)

            def second_half(y, t):
                act.wait_ge(s["ar"][y], t + 1)
                need(act, s["hw"][y], t)
                copy(ar_lo[y][:, :], ps_ar[y][:, AR:2 * AR]).then_inc(s["arlo"][y], 1)

            def exp_ratio(y, t):
                act.wait_ge(s["top"][y], t + 1)
                nc.scalar.activation(ratio[y][:, :], top[y][:, 0:1], ACT.Exp, scale=-1.0,
                                     bias=top[y][:, 1:2]).then_inc(s["ratio"][y], 1)

            def turned_hw(y, t):
                act.wait_ge(s["hwt"][y], t + 1)
                need(act, s["b"][y], t)
                copy(hwT[y][HI][:, :], ps_ar[y][:, HWT]).then_inc(s["hwh"][y], 1)

            def step(t, has):
                if has(0):
                    second_half(0, t)
                    exp_ratio(0, t)
                if has(-1):
                    act.wait_ge(s["mix"], t)
                    need(act, s["t1"], t - 1)
                    nc.scalar.activation(y1[:, :], ps_mix[:, :], ACT.Identity,
                                         bias=mix_bias[:, bass.ds(t - 1, 1)]).then_inc(s["y1"], 1)
                    act.wait_ge(s["t1"], t)
                    need(act, s["b"][1], t - 1)
                    copy(yT[1][HI][:, :, :].rearrange("p a b -> p (a b)"), ps_t1[:, :]).then_inc(s["yh"][1], 1)
                if has(0):
                    turned_hw(0, t)
                    if isinstance(t, int) and t == 0:
                        act.wait_ge(mixk_ready, C // 4)
                    need(act, s["mix"], t)
                    copy(mix_part[HI][:, :], mix[:, bass.ds(t * SPT, SPT), :].rearrange("p a b -> p (a b)")
                         ).then_inc(s["mh"], 1)
                if has(-1):
                    second_half(1, t - 1)
                    exp_ratio(1, t - 1)
                if has(0):
                    act.wait_ge(s["x1"], t + 1)
                    need(act, s["mix"], t)
                    copy(x1_part[HI][:, :], x1[:, :]).then_inc(s["x1h"], 1)
                if has(2):
                    split_x(t + 2)
                if has(1):
                    act.wait_ge(s["t0"], t + 2)
                    need(act, s["b"][0], t + 1)
                    copy(yT[0][HI][:, :, :].rearrange("p l (j o) -> p l j o", o=C),
                         ps_t0[:, :].rearrange("p (j l o) -> p l j o", j=SPT, l=PH)).then_inc(s["yh"][0], 1)
                if has(-1):
                    turned_hw(1, t - 1)
                if isinstance(t, int) and t == 0:
                    split_weights(1)
            stages(act, step)

        @block.vector
        def _(dve):
            v = nc.vector

            def low(dst, src, hi):
                return v.tensor_tensor(dst, src, hi, ALU.subtract)

            def low_weights(y):
                dve.wait_ge(w_hi[y], 1)
                low(ar_w[y][:, :, LO, :], ar_raw[y][:, :, :], ar_w[y][:, :, HI, :].bitcast(F32)).then_inc(w_lo[y], 1)
                dve.wait_ge(w_hi[y], 2)
                low(base_w[y][:, LO, :, :], base_raws[y][:, :, :],
                    base_w[y][:, HI, :, :].bitcast(F32)).then_inc(w_lo[y], 1)
                dve.wait_ge(w_hi[y], 3)
                low(lb_w[y][:, LO, :], lb_raw[y][:, :], lb_w[y][:, HI, :].bitcast(F32)).then_inc(w_lo[y], 1)

            dve.wait_ge(conv_w_hi, 1)
            low(conv_w[:, LO, :, :], conv_raw[:, :, :], conv_w[:, HI, :, :].bitcast(F32)).then_inc(conv_w_lo, 1)
            dve.wait_ge(cb_mm, 1)
            v.tensor_scalar(conv_bias[:, :], ps_mix[:, 0:N], side_sb[:, 0:1], None, ALU.add).then_inc(cb_ready, 1)

            def softmax_setup():
                dve.wait_ge(mlp_mm, 3)
                v.tensor_tensor(att[:, 0, :], ps_t1[:, 2 * N:2 * N + E], b2_sb[:, :], ALU.add).then_inc(mlp_dve, 1)
                dve.wait_ge(mlp_dve, 1)
                v.tensor_reduce(att_s[:, 0:1], att[:, 0, :], AX.X, ALU.max, negate=True).then_inc(mlp_dve, 1)
                dve.wait_ge(mlp_act, 3)
                v.reciprocal(att_s[:, 2:3], att_s[:, 1:2]).then_inc(mlp_dve, 1)
                dve.wait_ge(mlp_dve, 3)
                dve.wait_ge(l_const, 48)
                v.scalar_tensor_tensor(out=att_m[:, :, :], in0=att[:, 1:2, :].to_broadcast([P, SPT, E]),
                                       scalar=att_s[:, 2:3], in1=own[:, :, :], op0=ALU.mult,
                                       op1=ALU.mult).then_inc(mlp_dve, 1)

            def mixing_setup():
                dve.wait_ge(mlp_mm, 4)
                v.tensor_copy(att_mT[:, :], ps_t1[0:SPT * E, 0:N]).then_inc(mlp_dve, 1)
                dve.wait_ge(mlp_mm, 5)
                v.tensor_reduce(mix_bias[:, :], ps_t1[:, N:2 * N].rearrange("p (t j) -> p t j", j=SPT),
                                AX.X, ALU.add).then_inc(mixb_ready, 1)
                for q in range(C // 4):
                    dve.wait_ge(mixk_mm, q + 1)
                    ps = (ps_mix, ps_out[1])[q % 2]
                    v.tensor_copy(mix[:, :, 4 * q:4 * q + 4],
                                  ps[:, :].rearrange("p (c n) -> p n c", c=4)).then_inc(mixk_ready, 1)

            def route(y, t):
                def link(instruction):
                    instruction.then_inc(s["route"][y], 1)

                def done(n):
                    dve.wait_ge(s["route"][y], t * LINKS + n)

                dve.wait_ge(s["arlo"][y], t + 1)
                link(v.tensor_tensor(ar[y][:, ER:AR], ps_ar[y][:, ER:AR], ar_lo[y][:, ER:AR], ALU.add))
                done(1)
                link(v.tensor_tensor(ar[y][:, 0:ER], ps_ar[y][:, 0:ER], ar_lo[y][:, 0:ER], ALU.add))
                v.max(top[y][:, :], ar[y][:, ER:AR]).then_inc(s["top"][y], 1)
                dve.wait_ge(s["ratio"][y], t + 1)
                link(v.tensor_scalar(denom[y][:, :], ratio[y][:, :], 1.0 / SCALING, 1.0 / SCALING,
                                     ALU.mult, ALU.add))
                link(v.max_index(top_i[y][:, :], top[y][:, :], ar[y][:, ER:AR]))
                done(3)
                link(v.reciprocal(wts[y][:, 0:1], denom[y][:, :]))
                done(4)
                link(v.tensor_copy(top_f[y][:, :], top_i[y][:, 0:2]))
                done(5)
                link(v.tensor_tensor(wts[y][:, 1:2], ratio[y][:, :], wts[y][:, 0:1], ALU.mult))
                done(6)
                v.tensor_scalar(gates[y][:, 0, :], iota[:, :], top_f[y][:, 0:1], wts[y][:, 0:1],
                                ALU.is_equal, ALU.mult)
                done(7)
                link(v.tensor_scalar(gates[y][:, 1, :], iota[:, :], top_f[y][:, 1:2], wts[y][:, 1:2],
                                     ALU.is_equal, ALU.mult))
                done(8)
                link(v.tensor_tensor(gates[y][:, 2, :], gates[y][:, 0, :], gates[y][:, 1, :], ALU.add))
                done(9)
                v.tensor_tensor(hw[y][:, :].rearrange("p (e r) -> p e r", e=E),
                                ar[y][:, 0:ER].rearrange("p (e r) -> p e r", e=E),
                                gates[y][:, 2, :].unsqueeze(2).to_broadcast([P, E, R]),
                                ALU.mult).then_inc(s["hw"][y], 1)

            def turned_hw(y, t):
                dve.wait_ge(s["hwh"][y], t + 1)
                low(hwT[y][LO][:, :], ps_ar[y][:, HWT], hwT[y][HI][:, :].bitcast(F32)).then_inc(s["hwl"][y], 1)

            def step(t, has):
                if has(0):
                    route(0, t)
                if has(-2):
                    dve.wait_ge(s["b"][1], t - 1)
                    dve.wait_ge(s["x1b"], t - 1)
                    need(dve, stored, (t - 2) * 16)
                    v.tensor_tensor(res[:, :], ps_out[1][:, :], x1b[:, :], ALU.add).then_inc(s["out"], 1)
                if has(-1):
                    dve.wait_ge(s["yh"][1], t)
                    low(yT[1][LO][:, :, :].rearrange("p a b -> p (a b)"), ps_t1[:, :],
                        yT[1][HI][:, :, :].rearrange("p a b -> p (a b)").bitcast(F32)).then_inc(s["yl"][1], 1)
                if has(0):
                    turned_hw(0, t)
                if has(-1):
                    route(1, t - 1)
                if has(0):
                    dve.wait_ge(s["b"][0], t + 1)
                    dve.wait_ge(s["xb"], t + 1)
                    need(dve, s["x1h"], t)
                    need(dve, s["x1l"], t)
                    need(dve, s["x1b"], t)
                    v.tensor_tensor(x1[:, :], ps_out[0][:, :], xb[:, :], ALU.add).then_inc(s["x1"], 1)
                if isinstance(t, int) and t == 0:
                    mixing_setup()
                if has(1):
                    if isinstance(t, int) and t == -1:
                        dve.wait_ge(cb_ready, 1)
                    dve.wait_ge(s["conv"], t + 2)
                    need(dve, s["t0"], t + 1)
                    v.tensor_tensor(y0[:, :, :], ps_conv[:, :].rearrange("p (j b) -> p j b", j=SPT),
                                    conv_bias[:, bass.ds((t + 1) * SPT, SPT)].unsqueeze(2).to_broadcast([P, SPT, NB]),
                                    ALU.add).then_inc(s["y0"], 1)
                    if isinstance(t, int) and t == -1:
                        low_weights(0)
                        softmax_setup()
                    dve.wait_ge(s["yh"][0], t + 2)
                    low(yT[0][LO][:, :, :].rearrange("p l (j o) -> p l j o", o=C),
                        ps_t0[:, :].rearrange("p (j l o) -> p l j o", j=SPT, l=PH),
                        yT[0][HI][:, :, :].rearrange("p l (j o) -> p l j o", o=C).bitcast(F32)
                        ).then_inc(s["yl"][0], 1)
                if has(-1):
                    turned_hw(1, t - 1)
                if isinstance(t, int) and t == 0:
                    low_weights(1)
            stages(dve, step)

        @block.gpsimd
        def _(pool):
            g = nc.gpsimd

            def split_x(t):
                pool.wait_ge(s["xh"], t + 1)
                g.tensor_tensor(x_part[LO][:, :, :], x_raw[:, :, :], x_part[HI][:, :, :].bitcast(F32),
                                ALU.subtract).then_inc(s["xl"], 1)

            def step(t, has):
                if isinstance(t, int) and t == -1:
                    split_x(0)
                if has(-1):
                    if isinstance(t, int) and t == 1:
                        pool.wait_ge(l_bias[1], 16)
                    need(pool, s["out"], t - 1)
                    pool.wait_ge(s["x1"], t)
                    g.tensor_tensor(x1b[:, :], x1[:, :], bias[1][:, :], ALU.add).then_inc(s["x1b"], 1)
                if has(0):
                    if isinstance(t, int) and t == 0:
                        pool.wait_ge(l_bias[0], 16)
                    pool.wait_ge(tok_loaded, 16 * (t + 1))
                    need(pool, s["x1"], t)
                    g.tensor_tensor(xb[:, :], x_tok[:, :], bias[0][:, :], ALU.add).then_inc(s["xb"], 1)
                    pool.wait_ge(s["mh"], t + 1)
                    g.tensor_tensor(mix_part[LO][:, :],
                                    mix[:, bass.ds(t * SPT, SPT), :].rearrange("p a b -> p (a b)"),
                                    mix_part[HI][:, :].bitcast(F32), ALU.subtract).then_inc(s["ml"], 1)
                    pool.wait_ge(s["x1h"], t + 1)
                    g.tensor_tensor(x1_part[LO][:, :], x1[:, :], x1_part[HI][:, :].bitcast(F32),
                                    ALU.subtract).then_inc(s["x1l"], 1)
                if has(2):
                    split_x(t + 2)
            stages(pool, step)


def kernel(**inputs):
    import numpy as np
    import concourse.bacc as bacc
    from concourse.bass_utils import run_bass_kernel_spmd as run

    i = {k: np.asarray(v) for k, v in inputs.items()}
    x = i["x"]
    xp = np.zeros((TILES, C, PH, SPT, NBP), x.dtype)
    xp[..., 1:NB + 1] = x.reshape(TILES, SPT, C, NB, PH).transpose(0, 2, 4, 1, 3)
    w = i["L0_cond_weight"]
    cw = np.zeros((C, PH, SHIFTS, PH, C), w.dtype)
    cg = C // GROUPS
    for sh in range(SHIFTS):
        for pi in range(PH):
            for po in range(PH):
                k = PH * (sh - 1) + pi - po + TAPS // 2
                if 0 <= k < TAPS:
                    for q in range(GROUPS):
                        at = slice(q * cg, (q + 1) * cg)
                        cw[at, pi, sh, po, at] = w[at, :, k].T
    wk = i["L1_cond_weight"][..., 0]
    kern = np.zeros((SPT, E, C, SPT, C), wk.dtype)
    bk = np.zeros((SPT, E, SPT, C), wk.dtype)
    for j in range(SPT):
        kern[j, :, :, j, :] = wk
        bk[j, :, j, :] = i["L1_cond_bias_k"]

    def weights(layer, order):
        wb, a, r, b = (i[f"L{layer}_ffn_{n}"] for n in ("W_base", "A", "W_router", "B"))
        ar = np.concatenate([a.reshape(ER, D).T, r.T], axis=1)
        return {
            f"base{layer}": order(wb.T), f"ar{layer}": order(ar),
            f"lb{layer}": b.transpose(0, 2, 1).reshape(ER, D),
            f"bias{layer}": np.tile(i[f"L{layer}_ffn_b_base"], (P, 1)),
        }

    f = np.float32
    arrays = {
        "x_phase": xp.reshape(TILES, P, SPT, NBP),
        "x_tok": x.reshape(TILES, P, D),
        "conv_w": cw.reshape(P, SHIFTS, P),
        **weights(0, lambda a: a.reshape(P, KT, -1)),
        **weights(1, lambda a: a.reshape(KT, P, -1).transpose(1, 0, 2)),
        "condT": i["cond_128"].T,
        "cw": np.tile(i["L0_cond_c_weight"].T, (1, PH)),
        "side": np.tile(i["fside_S_0"], PH)[:, None],
        "W0": i["L1_cond_W0"], "W1": i["L1_cond_W1"], "W2": i["L1_cond_W2"],
        "b0": i["L1_cond_b0"][:, None], "b1": i["L1_cond_b1"][:, None],
        "b2": np.tile(i["L1_cond_b2"], (P, 1)),
        "kern": kern.reshape(SPT * E, C, P), "bk": bk.reshape(SPT * E, P),
        "ident": np.eye(P, dtype=f),
        "iota": np.tile(np.arange(E, dtype=f), (P, 1)),
        "own": np.repeat(np.tile(np.eye(SPT, dtype=f), (P // SPT, 1)), E, axis=1).reshape(P, SPT, E),
    }
    arrays = {k: np.ascontiguousarray(a) for k, a in arrays.items()}
    nc = bacc.Bacc("TRN2", target_bir_lowering=False, num_devices=1)
    d = {k: nc.dram_tensor(f"in_{k}", a.shape, F32, kind="ExternalInput").ap() for k, a in arrays.items()}
    d["out"] = nc.dram_tensor("out", (TILES, P, D), F32, kind="ExternalOutput").ap()
    build(nc, d)
    r = run(nc, [{f"in_{k}": a for k, a in arrays.items()}], core_ids=[0])
    return r.results[0]["out"].reshape(N, C, D)
```

```python
import numpy as np
import concourse.bass as bass
from concourse import mybir
from contextlib import ExitStack

F32 = mybir.dt.float32
F32R = mybir.dt.float32r
U32 = mybir.dt.uint32
ALU = mybir.AluOpType
ACT = mybir.ActivationFunctionType
AX = mybir.AxisListType

P = 128
N, C, D = 128, 32, 512
SPT = P // C
TILES = N // SPT
TAPS, GROUPS = 9, 4
PH = 8
NB = D // PH
NBP = NB + 1
SHIFTS = 2
HALVES = 2
CH = C // HALVES
HP = P // 2
KT = D // P
E, R = 8, 16
ER = E * R
AR = ER + E
SCALING = 2.0
HI, LO = 0, 1
PAIRS = [0, 2, 1, 3]
YH = [4, 1]
SPLITS = [(HI, HI), (HI, LO), (LO, HI)]
LINKS = 9

PACK = {"condT": N, "cw": HALVES * P, "W0": P, "W1": P, "W2": E, "side": HALVES, "b0": 1, "b1": 1,
        "b2": E, "ident": P, "iota": E, "own": SPT * E}


def build(nc, d):
    ctx = ExitStack()
    with ctx:
        def sb(name, shape, dt=F32):
            return ctx.enter_context(nc.sbuf_tensor(name, shape, dt))

        def bank(name):
            return ctx.enter_context(nc.psum_tensor(name, [P, 512], F32))

        def sem(name):
            return ctx.enter_context(nc.semaphore(name))

        conv_raw = sb("conv_raw", [P, HALVES, SHIFTS, P])
        conv_w = sb("conv_w", [P, 2, HALVES, SHIFTS, P], F32R)
        base_raw = [sb(f"base_raw{y}", [P, KT, D]) for y in range(2)]
        ar_raw = [sb(f"ar_raw{y}", [P, KT, AR]) for y in range(2)]
        lb_raw = [sb(f"lb_raw{y}", [P, D]) for y in range(2)]
        base_w = [sb(f"base_w{y}", [P, 2, KT, D], F32R) for y in range(2)]
        ar_w = [sb(f"ar_w{y}", [P, KT, 2, AR], F32R) for y in range(2)]
        lb_w = [sb(f"lb_w{y}", [P, 2, D], F32R) for y in range(2)]
        bias = [sb(f"bias{y}", [P, D]) for y in range(2)]
        pack = sb("pack", [P, sum(PACK.values())])
        at = dict(zip(PACK, np.cumsum([0, *PACK.values()])))
        condT, cw_sb, w0_sb, w1_sb, w2_sb, side_sb, b0_sb, b1_sb, b2_sb, ident, iota, own = (
            pack[:, int(at[k]):int(at[k]) + n] for k, n in PACK.items())
        conv_bias = sb("conv_bias", [P, HALVES, N])
        hid = sb("hid", [P, 2, N])
        att = sb("att", [P, 4, E])
        att_s = sb("att_s", [P, 4])
        att_m = sb("att_m", [P, SPT, E])
        att_mT = sb("att_mT", [SPT * E, N])
        kern_sb = sb("kern_sb", [SPT * E, C * C])
        bk_sb = sb("bk_sb", [SPT * E, P])
        mix_nat = sb("mix_nat", [P, C * C])
        mix = sb("mix", [P, N, C])
        mix_bias = sb("mix_bias", [P, TILES])
        x_raw = sb("x_raw", [P, HALVES, SPT, NBP])
        x_part = [sb(f"x_part{p}", [P, HALVES, SPT, NBP], F32R) for p in range(2)]
        x_tok = sb("x_tok", [P, D])
        xb = sb("xb", [P, D])
        y0 = sb("y0", [P, HALVES, SPT, NB])
        x1 = sb("x1", [P, D])
        x1b = sb("x1b", [P, D])
        x1_part = [sb(f"x1_part{p}", [P, D], F32R) for p in range(2)]
        mix_part = [sb(f"mix_part{p}", [P, P], F32R) for p in range(2)]
        y1 = sb("y1", [P, D])
        yT = [[sb(f"yT{y}_{p}", [P, KT, P], F32R) for p in range(2)] for y in range(2)]
        res = sb("res", [P, D])
        ar_lo = [sb(f"ar_lo{y}", [P, AR]) for y in range(2)]
        ar = [sb(f"ar{y}", [P, AR]) for y in range(2)]
        top = [sb(f"top{y}", [P, 8]) for y in range(2)]
        top_i = [sb(f"top_i{y}", [P, 8], U32) for y in range(2)]
        top_f = [sb(f"top_f{y}", [P, 2]) for y in range(2)]
        ratio = [sb(f"ratio{y}", [P, 1]) for y in range(2)]
        denom = [sb(f"denom{y}", [P, 1]) for y in range(2)]
        wts = [sb(f"wts{y}", [P, 2]) for y in range(2)]
        gates = [sb(f"gates{y}", [P, 3, E]) for y in range(2)]
        hw = [sb(f"hw{y}", [P, ER]) for y in range(2)]
        hwT = [[sb(f"hwT{y}_{p}", [P, P], F32R) for p in range(2)] for y in range(2)]

        ps_conv, ps_t0, ps_mix, ps_t1 = bank("ps_conv"), bank("ps_t0"), bank("ps_mix"), bank("ps_t1")
        ps_out = [bank("ps_out0"), bank("ps_out1")]
        ps_ar = [bank("ps_ar0"), bank("ps_ar1")]
        HWT = slice(2 * AR, 2 * AR + P)

        l_conv, l_base, l_ar, l_lb, l_bias = sem("l_conv"), [sem("l_base0"), sem("l_base1")], \
            [sem("l_ar0"), sem("l_ar1")], [sem("l_lb0"), sem("l_lb1")], [sem("l_bias0"), sem("l_bias1")]
        l_pack, l_kern = sem("l_pack"), sem("l_kern")
        x_loaded, tok_loaded, stored = sem("x_loaded"), sem("tok_loaded"), sem("stored")
        conv_w_hi, conv_w_lo = sem("conv_w_hi"), sem("conv_w_lo")
        w_hi = [sem("w_hi0"), sem("w_hi1")]
        w_lo = [sem("w_lo0"), sem("w_lo1")]
        cb_mm, cb_ready = sem("cb_mm"), sem("cb_ready")
        mlp_mm, mlp_act, mlp_dve = sem("mlp_mm"), sem("mlp_act"), sem("mlp_dve")
        mixk_mm, mixb_ready, mix_zero = sem("mixk_mm"), sem("mixb_ready"), sem("mix_zero")
        mix_nat_ready, mix_stored, mix_loaded = sem("mix_nat_ready"), sem("mix_stored"), sem("mix_loaded")
        names = ["xh", "xl", "xb", "conv", "y0", "t0", "x1", "x1h", "x1l", "x1b", "mh", "ml",
                 "mix", "y1", "t1", "out"]
        s = {n: sem("s_" + n) for n in names}
        for n in ["ar", "arlo", "top", "ratio", "hw", "hwt", "hwh", "hwl", "yh", "yl", "b", "route"]:
            s[n] = [sem(f"s_{n}{y}") for y in range(2)]

        def need(eng, semaphore, value):
            if isinstance(value, int) and value <= 0:
                return
            eng.wait_ge(semaphore, value)

        def stages(eng, step):
            def at(t):
                step(t, lambda k: 0 <= t + k < TILES)
            for t in range(-1, 3):
                at(t)
            with eng.Fori(3, TILES - 2) as t:
                step(t, lambda k: True)
            for t in range(TILES - 2, TILES + 2):
                at(t)

        def quarter(part, hi, sample):
            rows, tokens = slice(hi * HP, (hi + 1) * HP), slice(sample * HP, (sample + 1) * HP)
            return (yT[0][part][rows, :, tokens].rearrange("p k (m o) -> p k m o", o=CH),
                    ps_t0[tokens, :].rearrange("p (m l o) -> p l m o", m=SPT, l=PH)[:, hi * KT:(hi + 1) * KT])

        def mixing_half(q):
            return mix_nat[:, q * 512:(q + 1) * 512], (ps_mix, ps_out[1])[q][:, :]

        block = ctx.enter_context(nc.Block())

        @block.sync
        def _(sp):
            def load_x(t):
                need(sp, s["xh"], t)
                need(sp, s["xl"], t)
                sp.dma_start(x_raw[:, :, :, :], d["x_phase"][t]).then_inc(x_loaded, 16)

            def load_tok(t):
                need(sp, s["xb"], t)
                sp.dma_start(x_tok[:, :], d["x_tok"][t]).then_inc(tok_loaded, 16)

            sp.dma_start(pack[:, :], d["pack"]).then_inc(l_pack, 16)
            sp.dma_start(conv_raw[:, :, :, :], d["conv_w"]).then_inc(l_conv, 16)
            load_x(0)
            sp.dma_start(ar_raw[0][:, :, :], d["ar0"]).then_inc(l_ar[0], 16)
            sp.dma_start(base_raw[0][:, :, :], d["base0"]).then_inc(l_base[0], 16)
            sp.dma_start(kern_sb[:, :], d["kern"]).then_inc(l_kern, 16)
            sp.dma_start(bk_sb[:, :], d["bk"]).then_inc(l_kern, 16)
            sp.dma_start(lb_raw[0][:, :], d["lb0"]).then_inc(l_lb[0], 16)
            sp.dma_start(bias[0][:, :], d["bias0"]).then_inc(l_bias[0], 16)
            load_tok(0)
            load_x(1)
            sp.dma_start(ar_raw[1][:, :, :], d["ar1"]).then_inc(l_ar[1], 16)
            sp.dma_start(base_raw[1][:, :, :], d["base1"]).then_inc(l_base[1], 16)
            sp.dma_start(lb_raw[1][:, :], d["lb1"]).then_inc(l_lb[1], 16)
            sp.dma_start(bias[1][:, :], d["bias1"]).then_inc(l_bias[1], 16)
            sp.wait_ge(mix_nat_ready, 2)
            sp.dma_start(d["scratch"], mix_nat[:, :]).then_inc(mix_stored, 16)
            sp.wait_ge(mix_stored, 16)
            sp.wait_ge(mix_zero, 1)
            for j in range(SPT):
                sp.dma_start(mix[j * C:(j + 1) * C, j::SPT, :],
                             d["scratch"][j::SPT, :].rearrange("t (i o) -> i t o", o=C)).then_inc(mix_loaded, 16)

            def step(t, has):
                if has(0) and has(1):
                    load_tok(t + 1)
                if has(0) and has(2):
                    load_x(t + 2)
                if has(-2):
                    sp.wait_ge(s["out"], t - 1)
                    sp.dma_start(d["out"][t - 2], res[:, :]).then_inc(stored, 16)
            stages(sp, step)
            sp.wait_ge(stored, 16 * TILES)

        @block.tensor
        def _(pe):
            mm = nc.tensor.matmul

            def conv(t):
                if isinstance(t, int) and t == 0:
                    pe.wait_ge(conv_w_hi, 1)
                    pe.wait_ge(conv_w_lo, 1)
                need(pe, s["y0"], t)
                pe.wait_ge(s["xh"], t + 1)
                for h in range(HALVES):
                    for n, (dp, wp) in enumerate(SPLITS):
                        if h == 0 and dp == LO:
                            pe.wait_ge(s["xl"], t + 1)
                        for shift in range(SHIFTS):
                            last = mm(ps_conv[:, h * SPT * NB:(h + 1) * SPT * NB], conv_w[:, wp, h, shift, :],
                                      x_part[dp][:, h, :, shift:shift + NB], start=(n == 0 and shift == 0),
                                      stop=(n == len(SPLITS) - 1 and shift == SHIFTS - 1))
                last.then_inc(s["conv"], 1)

            def turn0(t):
                need(pe, s["yl"][0], t)
                pe.wait_ge(s["y0"], t + 1)
                for pair in range(SPT // 2):
                    for h in range(HALVES):
                        k = pair * HALVES + h
                        last = nc.tensor.transpose(ps_t0[:, k * P:(k + 1) * P], y0[:, h, 2 * pair:2 * pair + 2, :], ident)
                last.then_inc(s["t0"], 1)

            def turn1(t):
                need(pe, s["yl"][1], t)
                pe.wait_ge(s["y1"], t + 1)
                for k in range(KT):
                    last = nc.tensor.transpose(ps_t1[:, k * P:(k + 1) * P], y1[:, k * P:(k + 1) * P], ident)
                last.then_inc(s["t1"], 1)

            def ar_product(y, t):
                if isinstance(t, int) and t == 0:
                    pe.wait_ge(w_hi[y], 1)
                    pe.wait_ge(w_lo[y], 1)
                need(pe, s["hwl"][y], t)
                pe.wait_ge(s["yh"][y], (t + 1) * YH[y])
                for k in range(KT):
                    mm(ps_ar[y][:, 0:2 * AR], yT[y][HI][:, k, :],
                       ar_w[y][:, k, :, :].rearrange("p a b -> p (a b)"), start=(k == 0), stop=False,
                       skip_group_check=True)
                pe.wait_ge(s["yl"][y], t + 1)
                for k in range(KT):
                    last = mm(ps_ar[y][:, 0:AR], yT[y][LO][:, k, :], ar_w[y][:, k, HI, :],
                              start=False, stop=(k == KT - 1), skip_group_check=True)
                last.then_inc(s["ar"][y], 1)

            def base_product(y, t, ks):
                if 0 in ks:
                    if isinstance(t, int) and t == 0:
                        pe.wait_ge(w_hi[y], 2)
                        pe.wait_ge(w_lo[y], 2)
                    need(pe, s["x1"] if y == 0 else s["out"], t)
                for k in ks:
                    for n, (dp, wp) in enumerate(SPLITS):
                        mm(ps_out[y][:, :], yT[y][dp][:, k, :], base_w[y][:, wp, k, :],
                           start=(k == 0 and n == 0), stop=False)

            def turn_hw(y, t):
                pe.wait_ge(s["hw"][y], t + 1)
                nc.tensor.transpose(ps_ar[y][:, HWT], hw[y][:, :], ident).then_inc(s["hwt"][y], 1)

            def b_product(y, t):
                if isinstance(t, int) and t == 0:
                    pe.wait_ge(w_hi[y], 3)
                    pe.wait_ge(w_lo[y], 3)
                pe.wait_ge(s["hwh"][y], t + 1)
                for n, (dp, wp) in enumerate(SPLITS):
                    if dp == LO:
                        pe.wait_ge(s["hwl"][y], t + 1)
                    last = mm(ps_out[y][:, :], hwT[y][dp][:, :], lb_w[y][:, wp, :],
                              start=False, stop=(n == len(SPLITS) - 1))
                last.then_inc(s["b"][y], 1)

            def mix_product(t):
                need(pe, s["y1"], t)
                for p, q in ((s["x1h"], s["mh"]), (s["x1l"], s["ml"])):
                    pe.wait_ge(p, t + 1)
                    pe.wait_ge(q, t + 1)
                for n, (dp, wp) in enumerate(SPLITS):
                    last = mm(ps_mix[:, :], mix_part[wp][:, :], x1_part[dp][:, :],
                              start=(n == 0), stop=(n == len(SPLITS) - 1))
                last.then_inc(s["mix"], 1)

            pe.wait_ge(l_pack, 16)
            mm(ps_t1[:, 0:N], w0_sb, condT, start=True, stop=True).then_inc(mlp_mm, 1)
            for h in range(HALVES):
                last = mm(ps_mix[:, h * N:(h + 1) * N], cw_sb[:, h * P:(h + 1) * P], condT, start=True, stop=True)
            last.then_inc(cb_mm, 1)
            pe.wait_ge(mlp_act, 1)
            mm(ps_t1[:, N:2 * N], w1_sb, hid[:, 0, :], start=True, stop=True).then_inc(mlp_mm, 1)
            pe.wait_ge(mlp_act, 2)
            mm(ps_t1[:, 2 * N:2 * N + E], hid[:, 1, :], w2_sb, start=True, stop=True).then_inc(mlp_mm, 1)

            def turn_probabilities():
                pe.wait_ge(mlp_dve, 4)
                nc.tensor.transpose(ps_t1[0:SPT * E, 0:N], att_m[:, :, :].rearrange("p a b -> p (a b)"),
                                    ident).then_inc(mlp_mm, 1)

            def mixing_setup():
                pe.wait_ge(mlp_dve, 5)
                pe.wait_ge(l_kern, 32)
                mm(ps_t1[:, N:2 * N], bk_sb[:, :], att_mT[:, :], start=True, stop=True).then_inc(mlp_mm, 1)
                for q in range(2):
                    mm(mixing_half(q)[1], att_mT[:, :], kern_sb[:, q * 512:(q + 1) * 512],
                       start=True, stop=True).then_inc(mixk_mm, 1)

            def step(t, has):
                if has(0):
                    ar_product(0, t)
                if isinstance(t, int) and t == 0:
                    mixing_setup()
                if has(-2):
                    b_product(1, t - 2)
                if has(-1):
                    mix_product(t - 1)
                if has(0):
                    base_product(0, t, [0, 1])
                if has(-1):
                    turn1(t - 1)
                if has(0):
                    base_product(0, t, [2, 3])
                    turn_hw(0, t)
                if has(-1):
                    ar_product(1, t - 1)
                if has(1):
                    conv(t + 1)
                if has(0):
                    b_product(0, t)
                if has(-1):
                    base_product(1, t - 1, [0])
                if has(1):
                    turn0(t + 1)
                if isinstance(t, int) and t == -1:
                    turn_probabilities()
                if has(-1):
                    base_product(1, t - 1, [1, 2, 3])
                    turn_hw(1, t - 1)
            stages(pe, step)

        @block.scalar
        def _(act):
            def copy(dst, src):
                return nc.scalar.activation(dst, src, ACT.Copy)

            def split_x(t):
                act.wait_ge(x_loaded, 16 * (t + 1))
                need(act, s["conv"], t)
                copy(x_part[HI][:, :, :, :], x_raw[:, :, :, :]).then_inc(s["xh"], 1)

            def high_ar(y):
                act.wait_ge(l_ar[y], 16)
                copy(ar_w[y][:, :, HI, :], ar_raw[y][:, :, :]).then_inc(w_hi[y], 1)

            def high_base(y):
                act.wait_ge(l_base[y], 16)
                copy(base_w[y][:, HI, :, :], base_raw[y][:, :, :]).then_inc(w_hi[y], 1)

            def high_lb(y):
                act.wait_ge(l_lb[y], 16)
                copy(lb_w[y][:, HI, :], lb_raw[y][:, :]).then_inc(w_hi[y], 1)

            nc.scalar.preload_act_table(ACT.Gelu)
            act.wait_ge(l_pack, 16)
            act.wait_ge(mlp_mm, 1)
            nc.scalar.activation(hid[:, 0, :], ps_t1[:, 0:N], ACT.Gelu, bias=b0_sb).then_inc(mlp_act, 1)
            act.wait_ge(l_conv, 16)
            copy(conv_w[:, HI, :, :, :], conv_raw[:, :, :, :]).then_inc(conv_w_hi, 1)
            act.wait_ge(mlp_mm, 2)
            nc.scalar.activation(hid[:, 1, :], ps_t1[:, N:2 * N], ACT.Gelu, bias=b1_sb).then_inc(mlp_act, 1)
            split_x(0)
            high_ar(0)
            high_base(0)
            act.wait_ge(mlp_dve, 2)
            nc.scalar.activation(att[:, 1, :], att[:, 0, :], ACT.Exp, bias=att_s[:, 0:1],
                                 accum_out=att_s[:, 1:2]).then_inc(mlp_act, 1)

            def second_half(y, t):
                act.wait_ge(s["ar"][y], t + 1)
                need(act, s["hw"][y], t)
                copy(ar_lo[y][:, :], ps_ar[y][:, AR:2 * AR]).then_inc(s["arlo"][y], 1)

            def exp_ratio(y, t):
                act.wait_ge(s["top"][y], t + 1)
                nc.scalar.activation(ratio[y][:, :], top[y][:, 0:1], ACT.Exp, scale=-1.0,
                                     bias=top[y][:, 1:2]).then_inc(s["ratio"][y], 1)

            def turned_hw(y, t):
                act.wait_ge(s["hwt"][y], t + 1)
                need(act, s["b"][y], t)
                copy(hwT[y][HI][:, :], ps_ar[y][:, HWT]).then_inc(s["hwh"][y], 1)

            def step(t, has):
                if has(0):
                    second_half(0, t)
                    exp_ratio(0, t)
                if isinstance(t, int) and t == 0:
                    act.wait_ge(mixk_mm, 2)
                    copy(*mixing_half(1)).then_inc(mix_nat_ready, 1)
                if has(-1):
                    if isinstance(t, int) and t == 1:
                        act.wait_ge(mixb_ready, 1)
                    act.wait_ge(s["mix"], t)
                    need(act, s["t1"], t - 1)
                    nc.scalar.activation(y1[:, :], ps_mix[:, :], ACT.Identity,
                                         bias=mix_bias[:, bass.ds(t - 1, 1)]).then_inc(s["y1"], 1)
                    act.wait_ge(s["t1"], t)
                    need(act, s["b"][1], t - 1)
                    copy(yT[1][HI][:, :, :].rearrange("p a b -> p (a b)"), ps_t1[:, :]).then_inc(s["yh"][1], 1)
                if has(0):
                    turned_hw(0, t)
                    if isinstance(t, int) and t == 0:
                        high_ar(1)
                        high_base(1)
                        high_lb(1)
                        act.wait_ge(mix_loaded, 16 * SPT)
                    need(act, s["mix"], t)
                    copy(mix_part[HI][:, :], mix[:, bass.ds(t * SPT, SPT), :].rearrange("p a b -> p (a b)")
                         ).then_inc(s["mh"], 1)
                if has(-1):
                    second_half(1, t - 1)
                    exp_ratio(1, t - 1)
                if has(1):
                    act.wait_ge(s["t0"], t + 2)
                    need(act, s["b"][0], t + 1)
                    for sample in range(2):
                        for hi in range(2):
                            dst, src = quarter(HI, hi, sample)
                            copy(dst, src).then_inc(s["yh"][0], 1)
                if has(0):
                    act.wait_ge(s["x1"], t + 1)
                    need(act, s["mix"], t)
                    copy(x1_part[HI][:, :], x1[:, :]).then_inc(s["x1h"], 1)
                if has(2):
                    split_x(t + 2)
                if isinstance(t, int) and t == -1:
                    high_lb(0)
                if has(-1):
                    turned_hw(1, t - 1)
            stages(act, step)

        @block.vector
        def _(dve):
            v = nc.vector

            def low(dst, src, hi):
                return v.tensor_tensor(dst, src, hi, ALU.subtract)

            def low_ar(y):
                dve.wait_ge(w_hi[y], 1)
                low(ar_w[y][:, :, LO, :], ar_raw[y][:, :, :], ar_w[y][:, :, HI, :].bitcast(F32)).then_inc(w_lo[y], 1)

            def low_base(y):
                dve.wait_ge(w_hi[y], 2)
                low(base_w[y][:, LO, :, :], base_raw[y][:, :, :],
                    base_w[y][:, HI, :, :].bitcast(F32)).then_inc(w_lo[y], 1)

            def low_lb(y):
                dve.wait_ge(w_hi[y], 3)
                low(lb_w[y][:, LO, :], lb_raw[y][:, :], lb_w[y][:, HI, :].bitcast(F32)).then_inc(w_lo[y], 1)

            dve.wait_ge(conv_w_hi, 1)
            low(conv_w[:, LO, :, :, :], conv_raw[:, :, :, :],
                conv_w[:, HI, :, :, :].bitcast(F32)).then_inc(conv_w_lo, 1)
            dve.wait_ge(cb_mm, 1)
            dve.wait_ge(l_pack, 16)
            for h in range(HALVES):
                v.tensor_scalar(conv_bias[:, h, :].rearrange("p (t q a) -> p t a q", q=2, a=2),
                                ps_mix[:, h * N:(h + 1) * N].rearrange("p (t a q) -> p t a q", q=2, a=2),
                                side_sb[:, h:h + 1], None, ALU.add).then_inc(cb_ready, 1)

            def scores():
                dve.wait_ge(mlp_mm, 3)
                v.tensor_tensor(att[:, 0, :], ps_t1[:, 2 * N:2 * N + E], b2_sb, ALU.add).then_inc(mlp_dve, 1)
                dve.wait_ge(mlp_dve, 1)
                v.tensor_reduce(att_s[:, 0:1], att[:, 0, :], AX.X, ALU.max, negate=True).then_inc(mlp_dve, 1)

            def probabilities():
                dve.wait_ge(mlp_act, 3)
                v.reciprocal(att_s[:, 2:3], att_s[:, 1:2]).then_inc(mlp_dve, 1)
                dve.wait_ge(mlp_dve, 3)
                v.scalar_tensor_tensor(out=att_m[:, :, :], in0=att[:, 1:2, :].to_broadcast([P, SPT, E]),
                                       scalar=att_s[:, 2:3], in1=own.rearrange("p (j e) -> p j e", e=E), op0=ALU.mult,
                                       op1=ALU.mult).then_inc(mlp_dve, 1)

            def turned_probabilities():
                dve.wait_ge(mlp_mm, 4)
                v.tensor_copy(att_mT[:, :], ps_t1[0:SPT * E, 0:N]).then_inc(mlp_dve, 1)

            def mixing_setup():
                dve.wait_ge(mlp_mm, 5)
                v.tensor_reduce(mix_bias[:, :], ps_t1[:, N:2 * N].rearrange("p (t j) -> p t j", j=SPT),
                                AX.X, ALU.add).then_inc(mixb_ready, 1)
                dve.wait_ge(mixk_mm, 1)
                v.tensor_copy(*mixing_half(0)).then_inc(mix_nat_ready, 1)

            def route(y, t, meanwhile, before_gates):
                def link(instruction):
                    instruction.then_inc(s["route"][y], 1)

                def done(n):
                    dve.wait_ge(s["route"][y], t * LINKS + n)

                dve.wait_ge(s["arlo"][y], t + 1)
                link(v.tensor_tensor(ar[y][:, ER:AR], ps_ar[y][:, ER:AR], ar_lo[y][:, ER:AR], ALU.add))
                done(1)
                link(v.tensor_tensor(ar[y][:, 0:ER], ps_ar[y][:, 0:ER], ar_lo[y][:, 0:ER], ALU.add))
                v.max(top[y][:, :], ar[y][:, ER:AR]).then_inc(s["top"][y], 1)
                meanwhile()
                dve.wait_ge(s["ratio"][y], t + 1)
                link(v.tensor_scalar(denom[y][:, :], ratio[y][:, :], 1.0 / SCALING, 1.0 / SCALING,
                                     ALU.mult, ALU.add))
                link(v.max_index(top_i[y][:, :], top[y][:, :], ar[y][:, ER:AR]))
                done(3)
                link(v.reciprocal(wts[y][:, 0:1], denom[y][:, :]))
                done(4)
                link(v.tensor_copy(top_f[y][:, :], top_i[y][:, 0:2]))
                done(5)
                link(v.tensor_tensor(wts[y][:, 1:2], ratio[y][:, :], wts[y][:, 0:1], ALU.mult))
                before_gates()
                done(6)
                v.tensor_scalar(gates[y][:, 0, :], iota, top_f[y][:, 0:1], wts[y][:, 0:1],
                                ALU.is_equal, ALU.mult)
                done(7)
                link(v.tensor_scalar(gates[y][:, 1, :], iota, top_f[y][:, 1:2], wts[y][:, 1:2],
                                     ALU.is_equal, ALU.mult))
                done(8)
                link(v.tensor_tensor(gates[y][:, 2, :], gates[y][:, 0, :], gates[y][:, 1, :], ALU.add))
                done(9)
                v.tensor_tensor(hw[y][:, :].rearrange("p (e r) -> p e r", e=E),
                                ar[y][:, 0:ER].rearrange("p (e r) -> p e r", e=E),
                                gates[y][:, 2, :].unsqueeze(2).to_broadcast([P, E, R]),
                                ALU.mult).then_inc(s["hw"][y], 1)

            def turned_hw(y, t):
                dve.wait_ge(s["hwh"][y], t + 1)
                low(hwT[y][LO][:, :], ps_ar[y][:, HWT], hwT[y][HI][:, :].bitcast(F32)).then_inc(s["hwl"][y], 1)

            def result(t):
                dve.wait_ge(s["b"][1], t + 1)
                dve.wait_ge(s["x1b"], t + 1)
                need(dve, stored, t * 16)
                v.tensor_tensor(res[:, :], ps_out[1][:, :], x1b[:, :], ALU.add).then_inc(s["out"], 1)

            def middle(t):
                dve.wait_ge(s["b"][0], t + 1)
                dve.wait_ge(s["xb"], t + 1)
                need(dve, s["x1h"], t)
                need(dve, s["x1l"], t)
                need(dve, s["x1b"], t)
                v.tensor_tensor(x1[:, :], ps_out[0][:, :], xb[:, :], ALU.add).then_inc(s["x1"], 1)

            def conv_out(t):
                if isinstance(t, int) and t == 0:
                    dve.wait_ge(cb_ready, HALVES)
                dve.wait_ge(s["conv"], t + 1)
                need(dve, s["t0"], t)
                v.tensor_tensor(y0[:, :, :, :], ps_conv[:, :].rearrange("p (h j b) -> p h j b", h=HALVES, j=SPT),
                                conv_bias[:, :, bass.ds(t * SPT, SPT)].unsqueeze(3)
                                .to_broadcast([P, HALVES, SPT, NB]), ALU.add).then_inc(s["y0"], 1)

            def step(t, has):
                def meanwhile0():
                    if has(-2):
                        result(t - 2)
                    if isinstance(t, int) and t == 0:
                        mixing_setup()

                def meanwhile1():
                    if has(1):
                        conv_out(t + 1)

                def before_gates1():
                    if has(0):
                        middle(t)

                if has(0):
                    route(0, t, meanwhile0, lambda: None)
                else:
                    meanwhile0()
                if has(-1):
                    dve.wait_ge(s["yh"][1], t)
                    low(yT[1][LO][:, :, :].rearrange("p a b -> p (a b)"), ps_t1[:, :],
                        yT[1][HI][:, :, :].rearrange("p a b -> p (a b)").bitcast(F32)).then_inc(s["yl"][1], 1)
                if has(0):
                    turned_hw(0, t)
                if has(-1):
                    route(1, t - 1, meanwhile1, before_gates1)
                else:
                    if isinstance(t, int) and t == 0:
                        low_ar(1)
                    if isinstance(t, int) and t == -1:
                        scores()
                        low_ar(0)
                    meanwhile1()
                    before_gates1()
                    if isinstance(t, int) and t == -1:
                        probabilities()
                if has(1):
                    for sample in range(2):
                        dve.wait_ge(s["yh"][0], (t + 1) * YH[0] + 2 * sample + 2)
                        for hi in range(2):
                            dst, src = quarter(LO, hi, sample)
                            last = low(dst, src, quarter(HI, hi, sample)[0].bitcast(F32))
                    last.then_inc(s["yl"][0], 1)
                if isinstance(t, int) and t == -1:
                    turned_probabilities()
                    low_base(0)
                    low_lb(0)
                if isinstance(t, int) and t == 0:
                    low_base(1)
                    low_lb(1)
                if has(-1):
                    turned_hw(1, t - 1)
            stages(dve, step)

        @block.gpsimd
        def _(pool):
            g = nc.gpsimd

            def split_x(t):
                pool.wait_ge(s["xh"], t + 1)
                g.tensor_tensor(x_part[LO][:, :, :, :], x_raw[:, :, :, :], x_part[HI][:, :, :, :].bitcast(F32),
                                ALU.subtract).then_inc(s["xl"], 1)

            def step(t, has):
                if isinstance(t, int) and t == -1:
                    split_x(0)
                    g.memset(mix[:, :, :], 0.0).then_inc(mix_zero, 1)
                if has(-1):
                    if isinstance(t, int) and t == 1:
                        pool.wait_ge(l_bias[1], 16)
                    need(pool, s["out"], t - 1)
                    pool.wait_ge(s["x1"], t)
                    g.tensor_tensor(x1b[:, :], x1[:, :], bias[1][:, :], ALU.add).then_inc(s["x1b"], 1)
                if has(0):
                    if isinstance(t, int) and t == 0:
                        pool.wait_ge(l_bias[0], 16)
                    pool.wait_ge(tok_loaded, 16 * (t + 1))
                    need(pool, s["x1"], t)
                    g.tensor_tensor(xb[:, :], x_tok[:, :], bias[0][:, :], ALU.add).then_inc(s["xb"], 1)
                    pool.wait_ge(s["mh"], t + 1)
                    g.tensor_tensor(mix_part[LO][:, :],
                                    mix[:, bass.ds(t * SPT, SPT), :].rearrange("p a b -> p (a b)"),
                                    mix_part[HI][:, :].bitcast(F32), ALU.subtract).then_inc(s["ml"], 1)
                    pool.wait_ge(s["x1h"], t + 1)
                    g.tensor_tensor(x1_part[LO][:, :], x1[:, :], x1_part[HI][:, :].bitcast(F32),
                                    ALU.subtract).then_inc(s["x1l"], 1)
                if has(2):
                    split_x(t + 2)
            stages(pool, step)


def kernel(**inputs):
    import numpy as np
    import concourse.bacc as bacc
    from concourse.bass_utils import run_bass_kernel_spmd as run

    i = {k: np.asarray(v) for k, v in inputs.items()}
    x = i["x"]
    lead = TAPS // 2
    xp = np.zeros((TILES, SPT, HALVES, CH, NBP, PH), x.dtype)
    xp.reshape(TILES, SPT, HALVES, CH, NBP * PH)[..., lead:lead + D] = x.reshape(TILES, SPT, HALVES, CH, D)
    xp = xp.transpose(0, 3, 5, 2, 1, 4)[..., PAIRS, :]
    w = i["L0_cond_weight"]
    cw = np.zeros((CH, PH, HALVES, SHIFTS, PH, CH), w.dtype)
    cg = C // GROUPS
    for sh in range(SHIFTS):
        for pi in range(PH):
            for po in range(PH):
                k = PH * sh + pi - po
                if 0 <= k < TAPS:
                    for g in range(GROUPS):
                        h, q = divmod(g * cg, CH)
                        cw[q:q + cg, pi, h, sh, po, q:q + cg] = w[g * cg:(g + 1) * cg, :, k].T
    wk = i["L1_cond_weight"][..., 0]
    kern = np.tile(wk.transpose(0, 2, 1).reshape(E, C * C), (SPT, 1))
    bk = np.zeros((SPT, E, SPT, C), wk.dtype)
    for j in range(SPT):
        bk[j, :, j, :] = i["L1_cond_bias_k"]

    def weights(layer, order):
        wb, a, r, b = (i[f"L{layer}_ffn_{n}"] for n in ("W_base", "A", "W_router", "B"))
        ar = np.concatenate([a.reshape(ER, D).T, r.T], axis=1)
        return {
            f"base{layer}": order(wb.T), f"ar{layer}": order(ar),
            f"lb{layer}": b.transpose(0, 2, 1).reshape(ER, D),
            f"bias{layer}": np.tile(i[f"L{layer}_ffn_b_base"], (P, 1)),
        }

    f = np.float32
    halves = lambda a: np.concatenate([np.tile(a[..., h * CH:(h + 1) * CH], PH) for h in range(HALVES)], -1)
    pack = {
        "condT": i["cond_128"].T,
        "cw": halves(i["L0_cond_c_weight"].T),
        "W0": i["L1_cond_W0"], "W1": i["L1_cond_W1"], "W2": i["L1_cond_W2"],
        "side": halves(i["fside_S_0"]).reshape(HALVES, P).T,
        "b0": i["L1_cond_b0"][:, None], "b1": i["L1_cond_b1"][:, None],
        "b2": np.tile(i["L1_cond_b2"], (P, 1)),
        "ident": np.eye(P, dtype=f),
        "iota": np.tile(np.arange(E, dtype=f), (P, 1)),
        "own": np.repeat(np.tile(np.eye(SPT, dtype=f), (P // SPT, 1)), E, axis=1),
    }
    assert {k: a.shape[1] for k, a in pack.items()} == PACK
    arrays = {
        "x_phase": xp.reshape(TILES, P, HALVES, SPT, NBP),
        "x_tok": x.reshape(TILES, P, D),
        "conv_w": cw.reshape(P, HALVES, SHIFTS, P),
        **weights(0, lambda a: a.reshape(NB, 2, KT, -1).transpose(1, 0, 2, 3).reshape(P, KT, -1)),
        **weights(1, lambda a: a.reshape(KT, P, -1).transpose(1, 0, 2)),
        "pack": np.concatenate(list(pack.values()), axis=1),
        "kern": kern, "bk": bk.reshape(SPT * E, P),
    }
    arrays = {k: np.ascontiguousarray(a) for k, a in arrays.items()}
    nc = bacc.Bacc("TRN2", target_bir_lowering=False, num_devices=1)
    d = {k: nc.dram_tensor(f"in_{k}", a.shape, F32, kind="ExternalInput").ap() for k, a in arrays.items()}
    d["out"] = nc.dram_tensor("out", (TILES, P, D), F32, kind="ExternalOutput").ap()
    d["scratch"] = nc.dram_tensor("scratch", (N, C * C), F32, kind="Internal").ap()
    build(nc, d)
    r = run(nc, [{f"in_{k}": a for k, a in arrays.items()}], core_ids=[0])
    return r.results[0]["out"].reshape(N, C, D)
```

```python
import numpy as np
import concourse.bass as bass
from concourse import mybir
from contextlib import ExitStack

F32 = mybir.dt.float32
F32R = mybir.dt.float32r
U32 = mybir.dt.uint32
ALU = mybir.AluOpType
ACT = mybir.ActivationFunctionType
AX = mybir.AxisListType

P = 128
N, C, D = 128, 32, 512
SPT = P // C
TILES = N // SPT
TAPS, GROUPS = 9, 4
PH = 8
NB = D // PH
NBP = NB + 1
SHIFTS = 2
HALVES = 2
CH = C // HALVES
HP = P // 2
KT = D // P
E, R = 8, 16
ER = E * R
AR = ER + E
SCALING = 2.0
HI, LO = 0, 1
DH = D // 2
OUT = slice(AR, AR + DH)
PAIRS = [0, 2, 1, 3]
YH = [4, 1]
SPLITS = [(HI, HI), (HI, LO), (LO, HI)]
LAST = TILES - 1
LOOP_FROM = 3
UNROLL = 3
ROUNDS = (TILES - 2 - LOOP_FROM) // UNROLL
assert LOOP_FROM + ROUNDS * UNROLL == TILES - 2

LINKS = 10

PACK = {"condT": N, "cw": HALVES * P, "W0": P, "W1": P, "W2": E, "side": HALVES, "b0": 1, "b1": 1,
        "b2": E, "ident": P, "iota": E, "own": SPT * E}


def build(nc, d):
    ctx = ExitStack()
    with ctx:
        def sb(name, shape, dt=F32):
            return ctx.enter_context(nc.sbuf_tensor(name, shape, dt))

        def bank(name):
            return ctx.enter_context(nc.psum_tensor(name, [P, 512], F32))

        def sem(name):
            return ctx.enter_context(nc.semaphore(name))

        conv_raw = sb("conv_raw", [P, HALVES, SHIFTS, P])
        conv_w = sb("conv_w", [P, 2, HALVES, SHIFTS, P], F32R)
        wa_raw = [sb(f"wa_raw{y}", [P, KT, AR + DH]) for y in range(2)]
        wb_raw = [sb(f"wb_raw{y}", [P, KT, DH]) for y in range(2)]
        lb_raw = [sb(f"lb_raw{y}", [P, D]) for y in range(2)]
        wa = [sb(f"wa{y}", [P, 2, KT, AR + DH], F32R) for y in range(2)]
        wb = [sb(f"wb{y}", [P, 2, KT, DH], F32R) for y in range(2)]
        lb_w = [sb(f"lb_w{y}", [P, 2, D], F32R) for y in range(2)]
        bias = [sb(f"bias{y}", [P, D]) for y in range(2)]
        pack = sb("pack", [P, sum(PACK.values())])
        at = dict(zip(PACK, np.cumsum([0, *PACK.values()])))
        condT, cw_sb, w0_sb, w1_sb, w2_sb, side_sb, b0_sb, b1_sb, b2_sb, ident, iota, own = (
            pack[:, int(at[k]):int(at[k]) + n] for k, n in PACK.items())
        conv_bias = sb("conv_bias", [P, HALVES, N])
        hid = sb("hid", [P, 2, N])
        att = sb("att", [P, 4, E])
        att_s = sb("att_s", [P, 4])
        att_m = sb("att_m", [P, SPT, E])
        att_mT = sb("att_mT", [SPT * E, N])
        kern_sb = sb("kern_sb", [SPT * E, C * C])
        bk_sb = sb("bk_sb", [SPT * E, P])
        mix_nat = sb("mix_nat", [P, C * C])
        mix = sb("mix", [P, N, C])
        mix_bias = sb("mix_bias", [P, TILES])
        ones = sb("ones", [P, P])
        k_sums = sb("k_sums", [P, 2, AR + D])
        k_sum = sb("k_sum", [P, AR + D])
        column_sums = sb("column_sums", [P, AR + D])
        x_raw = sb("x_raw", [P, HALVES, SPT, NBP])
        x_part = [sb(f"x_part{p}", [P, HALVES, SPT, NBP], F32R) for p in range(2)]
        x_tok = sb("x_tok", [P, D])
        xb = sb("xb", [P, D])
        y0 = sb("y0", [P, HALVES, SPT, NB])
        x1 = sb("x1", [P, D])
        passed = sb("passed", [P, D])
        base_bias = sb("base_bias", [P, D])
        x1b = sb("x1b", [P, D])
        x1_part = [sb(f"x1_part{p}", [P, D], F32R) for p in range(2)]
        mix_part = sb("mix_part", [P, 2, P], F32R)
        cross = sb("cross", [P, KT, P])
        y1 = sb("y1", [P, KT, P])
        yT = [[sb(f"yT{y}_{p}", [P, KT, P], F32R) for p in range(2)] for y in range(2)]
        res = sb("res", [P, D])
        res_last = sb("res_last", [P, D])
        logits = [sb(f"logits{y}", [P, E]) for y in range(2)]
        lora = [sb(f"lora{y}", [P, ER]) for y in range(2)]
        top = [sb(f"top{y}", [P, 8]) for y in range(2)]
        top_i = [sb(f"top_i{y}", [P, 8], U32) for y in range(2)]
        top_f = [sb(f"top_f{y}", [P, 2]) for y in range(2)]
        ratio = [sb(f"ratio{y}", [P, 1]) for y in range(2)]
        denom = [sb(f"denom{y}", [P, 1]) for y in range(2)]
        wts = [sb(f"wts{y}", [P, 2]) for y in range(2)]
        gates = [sb(f"gates{y}", [P, 3, E]) for y in range(2)]
        hw = [sb(f"hw{y}", [P, ER]) for y in range(2)]
        hwT = [[sb(f"hwT{y}_{p}", [P, P], F32R) for p in range(2)] for y in range(2)]

        ps_conv, ps_t0 = bank("ps_conv"), bank("ps_t0")
        ps_mix = ctx.enter_context(nc.psum_tensor("ps_mix", [P, 2, 512], F32))
        ps_hwT = [ps_mix[:, 0, 0:P], ps_t0[:, 0:P]]
        ps_out = [ctx.enter_context(nc.psum_tensor(f"ps_out{y}", [P, 2, 512], F32)) for y in range(2)]

        l_wa, l_wb, l_lb, l_bias = ([sem(f"l_{n}{y}") for y in range(2)] for n in ("wa", "wb", "lb", "bias"))
        l_conv, l_pack, l_kern = sem("l_conv"), sem("l_pack"), sem("l_kern")
        x_loaded, tok_loaded, stored = sem("x_loaded"), sem("tok_loaded"), sem("stored")
        conv_w_hi, conv_w_lo = sem("conv_w_hi"), sem("conv_w_lo")
        w_hi = [sem("w_hi0"), sem("w_hi1")]
        w_lo = [sem("w_lo0"), sem("w_lo1")]
        zeros_ready, ones_ready = sem("zeros_ready"), sem("ones_ready")
        cb_mm, cb_ready = sem("cb_mm"), sem("cb_ready")
        mlp_mm, mlp_act, mlp_dve = sem("mlp_mm"), sem("mlp_act"), sem("mlp_dve")
        mixk_mm, mixb_ready, mix_zero = sem("mixk_mm"), sem("mixb_ready"), sem("mix_zero")
        k_summed, sums_mm, sums_ready = sem("k_summed"), sem("sums_mm"), sem("sums_ready")
        mix_nat_ready, mix_stored, mix_loaded = sem("mix_nat_ready"), sem("mix_stored"), sem("mix_loaded")
        names = ["xh", "xl", "xb", "conv", "y0", "t0", "x1", "x1h", "x1l", "x1b", "mh", "ml",
                 "mix", "cross", "y1", "passed", "bb", "out"]
        s = {n: sem("s_" + n) for n in names}
        for n in ["ar", "top", "ratio", "hw", "hwt", "hwh", "hwl", "yh", "yl", "base", "b", "route"]:
            s[n] = [sem(f"s_{n}{y}") for y in range(2)]

        def need(eng, semaphore, value):
            if isinstance(value, int) and value <= 0:
                return
            eng.wait_ge(semaphore, value)

        def stages(eng, step):
            def at(t):
                step(t, lambda k: 0 <= t + k < TILES)
            for t in range(1, LOOP_FROM):
                at(t)
            with eng.Fori(0, ROUNDS) as i:
                t = i * UNROLL + LOOP_FROM
                for j in range(UNROLL):
                    step(t + j, lambda k: True)
            at(LAST - 1)

        def out_banks(y, t):
            return ps_out[0] if isinstance(t, int) and t == LAST else ps_out[y]

        def quarter(part, hi, sample):
            rows, tokens = slice(hi * HP, (hi + 1) * HP), slice(sample * HP, (sample + 1) * HP)
            return (yT[0][part][rows, :, tokens].rearrange("p k (m o) -> p k m o", o=CH),
                    ps_t0[tokens, :].rearrange("p (m l o) -> p l m o", m=SPT, l=PH)[:, hi * KT:(hi + 1) * KT])

        def mixed(part):
            return ps_mix[:, :, :].rearrange("p b (k w t) -> p (b k) w t", w=2, t=P)[:, :, part, :]

        def mixing_half(q):
            return mix_nat[:, q * 512:(q + 1) * 512], (ps_mix[:, 0, :], ps_out[1][:, 1, :])[q]

        block = ctx.enter_context(nc.Block())

        @block.sync
        def _(sp):
            def load_x(t):
                need(sp, s["xh"], t)
                need(sp, s["xl"], t)
                sp.dma_start(x_raw[:, :, :, :], d["x_phase"][t]).then_inc(x_loaded, 16)

            def load_weights(y):
                sp.dma_start(wa_raw[y][:, :, :], d[f"wa{y}"]).then_inc(l_wa[y], 16)
                sp.dma_start(wb_raw[y][:, :, :], d[f"wb{y}"]).then_inc(l_wb[y], 16)

            def load_tok(t):
                need(sp, s["xb"], t)
                sp.dma_start(x_tok[:, :], d["x_tok"][t]).then_inc(tok_loaded, 16)

            sp.dma_start(conv_raw[:, :, :, :], d["conv_w"]).then_inc(l_conv, 16)
            load_x(0)
            sp.dma_start(pack[:, :], d["pack"]).then_inc(l_pack, 16)
            load_weights(0)
            sp.dma_start(kern_sb[:, :], d["kern"]).then_inc(l_kern, 16)
            sp.dma_start(bk_sb[:, :], d["bk"]).then_inc(l_kern, 16)
            sp.dma_start(lb_raw[0][:, :], d["lb0"]).then_inc(l_lb[0], 16)
            sp.dma_start(bias[0][:, :], d["bias0"]).then_inc(l_bias[0], 16)
            load_tok(0)
            load_x(1)
            load_weights(1)
            sp.wait_ge(mix_nat_ready, 2)
            sp.dma_start(d["scratch"], mix_nat[:, :]).then_inc(mix_stored, 16)
            load_x(2)
            sp.wait_ge(mix_stored, 16)
            sp.wait_ge(mix_zero, 1)
            for j in range(SPT):
                sp.dma_start(mix[j * C:(j + 1) * C, j::SPT, :],
                             d["scratch"][j::SPT, :].rearrange("t (i o) -> i t o", o=C)).then_inc(mix_loaded, 16)
            sp.dma_start(bias[1][:, :], d["bias1"]).then_inc(l_bias[1], 16)
            load_tok(1)
            sp.dma_start(lb_raw[1][:, :], d["lb1"]).then_inc(l_lb[1], 16)

            def store(t, result=res):
                sp.wait_ge(s["out"], t + 1)
                sp.dma_start(d["out"][t], result[:, :]).then_inc(stored, 16)

            def step(t, has):
                if has(2):
                    load_x(t + 2)
                if has(-2):
                    store(t - 2)
                load_tok(t + 1)
            stages(sp, step)
            store(LAST - 2)
            store(LAST - 1)
            store(LAST, res_last)
            sp.wait_ge(stored, 16 * TILES)

        @block.tensor
        def _(pe):
            mm = nc.tensor.matmul

            def conv(t):
                if isinstance(t, int) and t == 0:
                    pe.wait_ge(conv_w_hi, 1)
                    pe.wait_ge(conv_w_lo, 1)
                need(pe, s["y0"], t)
                pe.wait_ge(s["xh"], t + 1)
                for h in range(HALVES):
                    for n, (dp, wp) in enumerate(SPLITS):
                        if h == 0 and dp == LO:
                            pe.wait_ge(s["xl"], t + 1)
                        for shift in range(SHIFTS):
                            last = mm(ps_conv[:, h * SPT * NB:(h + 1) * SPT * NB], conv_w[:, wp, h, shift, :],
                                      x_part[dp][:, h, :, shift:shift + NB], start=(n == 0 and shift == 0),
                                      stop=(n == len(SPLITS) - 1 and shift == SHIFTS - 1))
                last.then_inc(s["conv"], 1)

            def turn0(t):
                need(pe, s["yl"][0], t)
                pe.wait_ge(s["y0"], t + 1)
                for pair in range(SPT // 2):
                    for h in range(HALVES):
                        k = pair * HALVES + h
                        last = nc.tensor.transpose(ps_t0[:, k * P:(k + 1) * P], y0[:, h, 2 * pair:2 * pair + 2, :], ident)
                last.then_inc(s["t0"], 1)

            def first_product(y, t, before_low=None):
                if isinstance(t, int) and t == 0:
                    pe.wait_ge(w_hi[y], 1)
                    pe.wait_ge(w_lo[y], 1)
                    if y == 1:
                        pe.wait_ge(sums_ready, 2)
                if not (y == 1 and isinstance(t, int) and t == LAST):
                    need(pe, s["x1"] if y == 0 else s["out"], t)
                pe.wait_ge(s["yh"][y], (t + 1) * YH[y])
                for n, (dp, wp) in enumerate(SPLITS):
                    if dp == LO:
                        if before_low:
                            before_low()
                        pe.wait_ge(s["yl"][y], t + 1)
                    for k in range(KT):
                        last = mm(out_banks(y, t)[:, 0, 0:AR + DH], yT[y][dp][:, k, :], wa[y][:, wp, k, :],
                                  start=(n == 0 and k == 0), stop=(n == len(SPLITS) - 1 and k == KT - 1),
                                  skip_group_check=True)
                last.then_inc(s["ar"][y], 1)

            def second_product(y, t):
                if isinstance(t, int) and t == 0:
                    pe.wait_ge(w_hi[y], 2)
                    pe.wait_ge(w_lo[y], 2)
                for n, (dp, wp) in enumerate(SPLITS):
                    for k in range(KT):
                        last = mm(out_banks(y, t)[:, 1, OUT], yT[y][dp][:, k, :], wb[y][:, wp, k, :],
                                  start=(n == 0 and k == 0), stop=False, skip_group_check=True)
                last.then_inc(s["base"][y], 1)

            def turn_hw(y, t):
                pe.wait_ge(s["hw"][y], t + 1)
                nc.tensor.transpose(ps_hwT[y], hw[y][:, :], ident).then_inc(s["hwt"][y], 1)

            def b_product(y, t):
                if isinstance(t, int) and t == 0:
                    pe.wait_ge(w_hi[y], 3)
                    pe.wait_ge(w_lo[y], 3)
                pe.wait_ge(s["hwh"][y], t + 1)
                for n, (dp, wp) in enumerate(SPLITS):
                    if dp == LO:
                        pe.wait_ge(s["hwl"][y], t + 1)
                    for half in range(2):
                        last = mm(out_banks(y, t)[:, half, OUT], hwT[y][dp][:, :],
                                  lb_w[y][:, wp, half * DH:(half + 1) * DH],
                                  start=False, stop=(n == len(SPLITS) - 1), skip_group_check=True)
                last.then_inc(s["b"][y], 1)

            def mix_product(t):
                need(pe, s["y1"], t)
                pe.wait_ge(s["mh"], t + 1)
                pe.wait_ge(s["ml"], t + 1)
                pe.wait_ge(s["x1h"], t + 1)
                pe.wait_ge(s["x1l"], t + 1)
                for k in range(KT):
                    b, c = divmod(k * 2 * P, 512)
                    mm(ps_mix[:, b, c:c + 2 * P], x1_part[HI][:, k * P:(k + 1) * P],
                       mix_part[:, :, :].rearrange("p a b -> p (a b)"), start=True, stop=False,
                       skip_group_check=True)
                    last = mm(ps_mix[:, b, c:c + P], x1_part[LO][:, k * P:(k + 1) * P], mix_part[:, HI, :],
                              start=False, stop=True, skip_group_check=True)
                last.then_inc(s["mix"], 1)

            def keep_busy(count):
                pe.wait_ge(zeros_ready, 1)
                for _ in range(count):
                    mm(ps_out[0][:, 0, :], x1_part[HI][:, 0:P], x1_part[HI][:, :], start=True, stop=True)

            keep_busy(10)
            pe.wait_ge(l_pack, 16)
            mm(ps_mix[:, 1, 0:N], w0_sb, condT, start=True, stop=True).then_inc(mlp_mm, 1)
            for h in range(HALVES):
                last = mm(ps_mix[:, 0, h * N:(h + 1) * N], cw_sb[:, h * P:(h + 1) * P], condT, start=True, stop=True)
            last.then_inc(cb_mm, 1)
            pe.wait_ge(mlp_act, 1)
            mm(ps_mix[:, 1, N:2 * N], w1_sb, hid[:, 0, :], start=True, stop=True).then_inc(mlp_mm, 1)

            def kernel_scores():
                pe.wait_ge(mlp_act, 2)
                mm(ps_mix[:, 1, 2 * N:2 * N + E], hid[:, 1, :], w2_sb, start=True, stop=True).then_inc(mlp_mm, 1)

            def turn_probabilities():
                pe.wait_ge(mlp_dve, 4)
                nc.tensor.transpose(ps_mix[0:SPT * E, 1, 0:N], att_m[:, :, :].rearrange("p a b -> p (a b)"),
                                    ident).then_inc(mlp_mm, 1)

            def mixing_setup():
                pe.wait_ge(mlp_dve, 5)
                pe.wait_ge(l_kern, 32)
                mm(ps_mix[:, 1, N:2 * N], bk_sb[:, :], att_mT[:, :], start=True, stop=True).then_inc(mlp_mm, 1)
                for q in range(2):
                    mm(mixing_half(q)[1], att_mT[:, :], kern_sb[:, q * 512:(q + 1) * 512],
                       start=True, stop=True).then_inc(mixk_mm, 1)

            def step(t, has):
                first_product(0, t)
                mix_product(t - 1)
                if has(-2):
                    turn_hw(1, t - 2)
                second_product(0, t)
                if has(-2):
                    b_product(1, t - 2)
                conv(t + 1)
                first_product(1, t - 1, before_low=lambda: turn_hw(0, t))
                turn0(t + 1)
                b_product(0, t)
                second_product(1, t - 1)

            conv(0)
            kernel_scores()
            turn0(0)
            keep_busy(4)
            turn_probabilities()
            keep_busy(2)
            mixing_setup()
            first_product(0, 0)
            conv(1)
            second_product(0, 0)
            turn_hw(0, 0)
            turn0(1)
            b_product(0, 0)
            pe.wait_ge(ones_ready, 1)
            pe.wait_ge(k_summed, 3)
            pe.wait_ge(mix_nat_ready, 2)
            mm(ps_out[1][:, 0, 0:AR + DH], ones[:, :], k_sum[:, 0:AR + DH], start=True, stop=True)
            mm(ps_out[1][:, 1, OUT], ones[:, :], k_sum[:, AR + DH:AR + D], start=True, stop=True).then_inc(sums_mm, 1)
            stages(pe, step)
            first_product(0, LAST)
            mix_product(LAST - 1)
            turn_hw(1, LAST - 2)
            second_product(0, LAST)
            b_product(1, LAST - 2)
            pe.wait_ge(s["y1"], LAST)
            turn_hw(0, LAST)
            b_product(0, LAST)
            first_product(1, LAST - 1)
            mix_product(LAST)
            second_product(1, LAST - 1)
            first_product(1, LAST, before_low=lambda: turn_hw(1, LAST - 1))
            b_product(1, LAST - 1)
            second_product(1, LAST)
            turn_hw(1, LAST)
            b_product(1, LAST)

        @block.scalar
        def _(act):
            def copy(dst, src):
                return nc.scalar.activation(dst, src, ACT.Copy)

            def split_x(t):
                act.wait_ge(x_loaded, 16 * (t + 1))
                need(act, s["conv"], t)
                copy(x_part[HI][:, :, :, :], x_raw[:, :, :, :]).then_inc(s["xh"], 1)

            def high_wa(y):
                act.wait_ge(l_wa[y], 16)
                copy(wa[y][:, HI, :, :], wa_raw[y][:, :, :]).then_inc(w_hi[y], 1)

            def high_wb(y):
                act.wait_ge(l_wb[y], 16)
                copy(wb[y][:, HI, :, :], wb_raw[y][:, :, :]).then_inc(w_hi[y], 1)

            def high_lb(y):
                act.wait_ge(l_lb[y], 16)
                copy(lb_w[y][:, HI, :], lb_raw[y][:, :]).then_inc(w_hi[y], 1)

            nc.scalar.preload_act_table(ACT.Gelu)
            act.wait_ge(l_conv, 16)
            copy(conv_w[:, HI, :, :, :], conv_raw[:, :, :, :]).then_inc(conv_w_hi, 1)
            split_x(0)
            act.wait_ge(l_pack, 16)
            act.wait_ge(mlp_mm, 1)
            nc.scalar.activation(hid[:, 0, :], ps_mix[:, 1, 0:N], ACT.Gelu, bias=b0_sb).then_inc(mlp_act, 1)
            act.wait_ge(mlp_mm, 2)
            nc.scalar.activation(hid[:, 1, :], ps_mix[:, 1, N:2 * N], ACT.Gelu, bias=b1_sb).then_inc(mlp_act, 1)
            high_wa(0)
            act.wait_ge(mlp_dve, 2)
            nc.scalar.activation(att[:, 1, :], att[:, 0, :], ACT.Exp, bias=att_s[:, 0:1],
                                 accum_out=att_s[:, 1:2]).then_inc(mlp_act, 1)

            def exp_ratio(y, t):
                act.wait_ge(s["top"][y], t + 1)
                nc.scalar.activation(ratio[y][:, :], top[y][:, 0:1], ACT.Exp, scale=-1.0,
                                     bias=top[y][:, 1:2]).then_inc(s["ratio"][y], 1)

            def turned0(t, sample):
                act.wait_ge(s["t0"], t + 1)
                need(act, s["base"][0], t)
                for hi in range(2):
                    dst, src = quarter(HI, hi, sample)
                    copy(dst, src).then_inc(s["yh"][0], 1)

            def split_x1(t):
                act.wait_ge(s["x1"], t + 1)
                need(act, s["mix"], t)
                copy(x1_part[HI][:, :], x1[:, :]).then_inc(s["x1h"], 1)

            def save_sums():
                act.wait_ge(sums_mm, 1)
                copy(column_sums[:, 0:AR + DH], ps_out[1][:, 0, 0:AR + DH]).then_inc(sums_ready, 1)
                copy(column_sums[:, AR + DH:AR + D], ps_out[1][:, 1, OUT]).then_inc(sums_ready, 1)

            def pass_bias(t):
                if isinstance(t, int) and t == 0:
                    act.wait_ge(sums_ready, 2)
                    act.wait_ge(mixb_ready, 1)
                need(act, s["bb"], t)
                nc.scalar.activation(passed[:, :], column_sums[:, AR:AR + D], ACT.Copy,
                                     scale=mix_bias[:, bass.ds(t, 1)]).then_inc(s["passed"], 1)

            def split_mix(t):
                need(act, s["mix"], t)
                copy(mix_part[:, HI, :], mix[:, bass.ds(t * SPT, SPT), :].rearrange("p a b -> p (a b)")
                     ).then_inc(s["mh"], 1)

            def turned_hw(y, t):
                act.wait_ge(s["hwt"][y], t + 1)
                need(act, s["b"][y], t)
                copy(hwT[y][HI][:, :], ps_hwT[y]).then_inc(s["hwh"][y], 1)

            def save_cross(t):
                act.wait_ge(s["mix"], t + 1)
                need(act, s["y1"], t)
                copy(cross[:, :, :], mixed(1)).then_inc(s["cross"], 1)

            def turned1(t):
                act.wait_ge(s["y1"], t + 1)
                need(act, s["base"][1], t)
                copy(yT[1][HI][:, :, :], y1[:, :, :]).then_inc(s["yh"][1], 1)

            def step(t, has):
                exp_ratio(0, t)
                if has(-2):
                    turned_hw(1, t - 2)
                save_cross(t - 1)
                if isinstance(t, int) and t == 1:
                    save_sums()
                    pass_bias(0)
                turned1(t - 1)
                split_mix(t)
                if isinstance(t, int) and t == 1:
                    high_wb(1)
                    high_lb(1)
                if has(2):
                    split_x(t + 2)
                turned_hw(0, t)
                turned0(t + 1, 0)
                exp_ratio(1, t - 1)
                turned0(t + 1, 1)
                split_x1(t)
                pass_bias(t)

            turned0(0, 0)
            turned0(0, 1)
            high_wb(0)
            high_lb(0)
            split_x(1)
            act.wait_ge(mixk_mm, 2)
            copy(*mixing_half(1)).then_inc(mix_nat_ready, 1)
            exp_ratio(0, 0)
            high_wa(1)
            turned_hw(0, 0)
            turned0(1, 0)
            turned0(1, 1)
            split_x1(0)
            act.wait_ge(mix_loaded, 16 * SPT)
            split_mix(0)
            split_x(2)
            stages(act, step)
            exp_ratio(0, LAST)
            turned_hw(1, LAST - 2)
            save_cross(LAST - 1)
            turned1(LAST - 1)
            split_mix(LAST)
            turned_hw(0, LAST)
            split_x1(LAST)
            pass_bias(LAST)
            exp_ratio(1, LAST - 1)
            save_cross(LAST)
            turned1(LAST)
            turned_hw(1, LAST - 1)
            exp_ratio(1, LAST)
            turned_hw(1, LAST)

        @block.vector
        def _(dve):
            v = nc.vector

            def low(dst, src, hi):
                return v.tensor_tensor(dst, src, hi, ALU.subtract)

            def low_wa_part(y, ks):
                dve.wait_ge(w_hi[y], 1)
                return low(wa[y][:, LO, ks, :], wa_raw[y][:, ks, :], wa[y][:, HI, ks, :].bitcast(F32))

            def low_wa(y):
                low_wa_part(y, slice(0, KT)).then_inc(w_lo[y], 1)

            def low_wb(y):
                dve.wait_ge(w_hi[y], 2)
                low(wb[y][:, LO, :, :], wb_raw[y][:, :, :], wb[y][:, HI, :, :].bitcast(F32)).then_inc(w_lo[y], 1)

            def low_lb(y):
                dve.wait_ge(w_hi[y], 3)
                low(lb_w[y][:, LO, :], lb_raw[y][:, :], lb_w[y][:, HI, :].bitcast(F32)).then_inc(w_lo[y], 1)

            v.memset(x1_part[HI][:, :].bitcast(F32), 0.0).then_inc(zeros_ready, 1)
            dve.wait_ge(conv_w_hi, 1)
            low(conv_w[:, LO, :, :, :], conv_raw[:, :, :, :],
                conv_w[:, HI, :, :, :].bitcast(F32)).then_inc(conv_w_lo, 1)
            dve.wait_ge(s["xh"], 1)
            low(x_part[LO][:, :, :, :], x_raw[:, :, :, :], x_part[HI][:, :, :, :].bitcast(F32)).then_inc(s["xl"], 1)
            dve.wait_ge(cb_mm, 1)
            dve.wait_ge(l_pack, 16)
            for h in range(HALVES):
                v.tensor_scalar(conv_bias[:, h, :].rearrange("p (t q a) -> p t a q", q=2, a=2),
                                ps_mix[:, 0, h * N:(h + 1) * N].rearrange("p (t a q) -> p t a q", q=2, a=2),
                                side_sb[:, h:h + 1], None, ALU.add).then_inc(cb_ready, 1)

            def scores():
                dve.wait_ge(mlp_mm, 3)
                v.tensor_tensor(att[:, 0, :], ps_mix[:, 1, 2 * N:2 * N + E], b2_sb, ALU.add).then_inc(mlp_dve, 1)
                dve.wait_ge(mlp_dve, 1)
                v.tensor_reduce(att_s[:, 0:1], att[:, 0, :], AX.X, ALU.max, negate=True).then_inc(mlp_dve, 1)

            def probabilities():
                dve.wait_ge(mlp_act, 3)
                v.reciprocal(att_s[:, 2:3], att_s[:, 1:2]).then_inc(mlp_dve, 1)
                dve.wait_ge(mlp_dve, 3)
                v.scalar_tensor_tensor(out=att_m[:, :, :], in0=att[:, 1:2, :].to_broadcast([P, SPT, E]),
                                       scalar=att_s[:, 2:3], in1=own.rearrange("p (j e) -> p j e", e=E), op0=ALU.mult,
                                       op1=ALU.mult).then_inc(mlp_dve, 1)

            def turned_probabilities():
                dve.wait_ge(mlp_mm, 4)
                v.tensor_copy(att_mT[:, :], ps_mix[0:SPT * E, 1, 0:N]).then_inc(mlp_dve, 1)

            def mixing_setup():
                dve.wait_ge(mixk_mm, 1)
                v.tensor_copy(*mixing_half(0)).then_inc(mix_nat_ready, 1)
                v.tensor_reduce(mix_bias[:, :], ps_mix[:, 1, N:2 * N].rearrange("p (t j) -> p t j", j=SPT),
                                AX.X, ALU.add).then_inc(mixb_ready, 1)

            def route(y, t, meanwhile=None, before_weights=None, before_sum=None):
                def link(instruction):
                    instruction.then_inc(s["route"][y], 1)

                def leave(dst, first, end):
                    if y == 0:
                        return v.tensor_copy(dst, ps_out[0][:, 0, first:end])
                    return v.scalar_tensor_tensor(out=dst, in0=column_sums[:, first:end],
                                                  scalar=mix_bias[:, bass.ds(t, 1)],
                                                  in1=out_banks(1, t)[:, 0, first:end], op0=ALU.mult, op1=ALU.add)

                def done(n):
                    dve.wait_ge(s["route"][y], t * LINKS + n)

                dve.wait_ge(s["ar"][y], t + 1)
                if y == 1 and isinstance(t, int) and t == 0:
                    dve.wait_ge(sums_ready, 1)
                link(leave(logits[y][:, :], ER, AR))
                done(1)
                link(leave(lora[y][:, 0:HP], 0, HP))
                v.max(top[y][:, :], logits[y][:, :]).then_inc(s["top"][y], 1)
                dve.wait_ge(s["top"][y], t + 1)
                link(leave(lora[y][:, HP:ER], HP, ER))
                link(v.max_index(top_i[y][:, :], top[y][:, :], logits[y][:, :]))
                if meanwhile:
                    meanwhile()
                dve.wait_ge(s["ratio"][y], t + 1)
                link(v.tensor_scalar(denom[y][:, :], ratio[y][:, :], 1.0 / SCALING, 1.0 / SCALING,
                                     ALU.mult, ALU.add))
                done(4)
                link(v.tensor_copy(top_f[y][:, :], top_i[y][:, 0:2]))
                if before_weights:
                    before_weights()
                done(5)
                link(v.reciprocal(wts[y][:, 0:1], denom[y][:, :]))
                done(7)
                link(v.tensor_tensor(wts[y][:, 1:2], ratio[y][:, :], wts[y][:, 0:1], ALU.mult))
                v.tensor_scalar(gates[y][:, 0, :], iota, top_f[y][:, 0:1], wts[y][:, 0:1],
                                ALU.is_equal, ALU.mult)
                done(8)
                link(v.tensor_scalar(gates[y][:, 1, :], iota, top_f[y][:, 1:2], wts[y][:, 1:2],
                                     ALU.is_equal, ALU.mult))
                if before_sum:
                    before_sum()
                done(9)
                link(v.tensor_tensor(gates[y][:, 2, :], gates[y][:, 0, :], gates[y][:, 1, :], ALU.add))
                done(10)
                v.tensor_tensor(hw[y][:, :].rearrange("p (e r) -> p e r", e=E),
                                lora[y][:, :].rearrange("p (e r) -> p e r", e=E),
                                gates[y][:, 2, :].unsqueeze(2).to_broadcast([P, E, R]),
                                ALU.mult).then_inc(s["hw"][y], 1)

            def turned_hw(y, t):
                dve.wait_ge(s["hwh"][y], t + 1)
                low(hwT[y][LO][:, :], ps_hwT[y], hwT[y][HI][:, :].bitcast(F32)).then_inc(s["hwl"][y], 1)

            def halves(features):
                return features[:, :].rearrange("p (h d) -> p h d", h=2)

            def result(t):
                dve.wait_ge(s["b"][1], t + 1)
                dve.wait_ge(s["x1b"], t + 1)
                need(dve, stored, t * 16)
                v.tensor_tensor(halves(res), ps_out[1][:, :, OUT], halves(x1b), ALU.add).then_inc(s["out"], 1)

            def last_result():
                dve.wait_ge(s["b"][1], LAST + 1)
                dve.wait_ge(s["x1b"], LAST + 1)
                v.tensor_tensor(halves(res_last), out_banks(1, LAST)[:, :, OUT], halves(base_bias),
                                ALU.add).then_inc(s["out"], 1)

            def middle(t):
                dve.wait_ge(s["b"][0], t + 1)
                dve.wait_ge(s["xb"], t + 1)
                need(dve, s["x1h"], t)
                need(dve, s["x1l"], t)
                need(dve, s["x1b"], t)
                v.tensor_tensor(halves(x1), ps_out[0][:, :, OUT], halves(xb), ALU.add).then_inc(s["x1"], 1)

            def conv_out(t):
                if isinstance(t, int) and t == 0:
                    dve.wait_ge(cb_ready, HALVES)
                dve.wait_ge(s["conv"], t + 1)
                need(dve, s["t0"], t)
                v.tensor_tensor(y0[:, :, :, :], ps_conv[:, :].rearrange("p (h j b) -> p h j b", h=HALVES, j=SPT),
                                conv_bias[:, :, bass.ds(t * SPT, SPT)].unsqueeze(3)
                                .to_broadcast([P, HALVES, SPT, NB]), ALU.add).then_inc(s["y0"], 1)

            def turned0(t):
                for sample in range(2):
                    dve.wait_ge(s["yh"][0], t * YH[0] + 2 * sample + 2)
                    for hi in range(2):
                        dst, src = quarter(LO, hi, sample)
                        last = low(dst, src, quarter(HI, hi, sample)[0].bitcast(F32))
                last.then_inc(s["yl"][0], 1)

            def sum_mixed(t):
                dve.wait_ge(s["cross"], t + 1)
                need(dve, s["yh"][1], t)
                need(dve, s["yl"][1], t)
                v.tensor_tensor(y1[:, :, :], mixed(0), cross[:, :, :], ALU.add).then_inc(s["y1"], 1)

            def turned1(t):
                dve.wait_ge(s["yh"][1], t + 1)
                low(yT[1][LO][:, :, :], y1[:, :, :], yT[1][HI][:, :, :].bitcast(F32)).then_inc(s["yl"][1], 1)

            def step(t, has):
                def previous_tiles():
                    if has(-2):
                        turned_hw(1, t - 2)
                    sum_mixed(t - 1)

                def previous_result():
                    if has(-2):
                        result(t - 2)

                def tiles_ends():
                    middle(t)
                    turned0(t + 1)

                route(0, t, before_weights=previous_tiles, before_sum=previous_result)
                turned1(t - 1)
                conv_out(t + 1)
                if isinstance(t, int) and t == 1:
                    low_wb(1)
                turned_hw(0, t)
                route(1, t - 1, meanwhile=tiles_ends)
                if isinstance(t, int) and t == 1:
                    low_lb(1)

            conv_out(0)
            scores()
            low_wa_part(0, slice(0, KT // 2))
            probabilities()
            turned_probabilities()
            low_wa_part(0, slice(KT // 2, KT)).then_inc(w_lo[0], 1)
            mixing_setup()
            turned0(0)
            low_wb(0)
            route(0, 0)
            conv_out(1)
            low_lb(0)
            turned_hw(0, 0)
            middle(0)
            turned0(1)
            low_wa(1)
            stages(dve, step)

            def mixing_before_last():
                turned_hw(1, LAST - 2)
                sum_mixed(LAST - 1)

            route(0, LAST, before_weights=mixing_before_last)
            result(LAST - 2)
            turned_hw(0, LAST)
            middle(LAST)
            turned1(LAST - 1)
            dve.wait_ge(s["x1h"], LAST + 1)
            low(x1_part[LO][:, :], x1[:, :], x1_part[HI][:, :].bitcast(F32)).then_inc(s["x1l"], 1)
            route(1, LAST - 1, before_weights=lambda: sum_mixed(LAST))
            turned1(LAST)
            turned_hw(1, LAST - 1)
            route(1, LAST)
            result(LAST - 1)
            turned_hw(1, LAST)
            last_result()

        @block.gpsimd
        def _(pool):
            g = nc.gpsimd

            def split_x(t):
                pool.wait_ge(s["xh"], t + 1)
                g.tensor_tensor(x_part[LO][:, :, :, :], x_raw[:, :, :, :], x_part[HI][:, :, :, :].bitcast(F32),
                                ALU.subtract).then_inc(s["xl"], 1)

            def split_mix(t):
                pool.wait_ge(s["mh"], t + 1)
                g.tensor_tensor(mix_part[:, LO, :], mix[:, bass.ds(t * SPT, SPT), :].rearrange("p a b -> p (a b)"),
                                mix_part[:, HI, :].bitcast(F32), ALU.subtract).then_inc(s["ml"], 1)

            def form_xb(t):
                pool.wait_ge(tok_loaded, 16 * (t + 1))
                need(pool, s["x1"], t)
                g.tensor_tensor(xb[:, :], x_tok[:, :], bias[0][:, :], ALU.add).then_inc(s["xb"], 1)

            def split_x1(t):
                pool.wait_ge(s["x1h"], t + 1)
                g.tensor_tensor(x1_part[LO][:, :], x1[:, :], x1_part[HI][:, :].bitcast(F32),
                                ALU.subtract).then_inc(s["x1l"], 1)

            def form_base_bias(t):
                pool.wait_ge(s["passed"], t + 1)
                need(pool, s["x1b"], t)
                g.tensor_tensor(base_bias[:, :], passed[:, :], bias[1][:, :], ALU.add).then_inc(s["bb"], 1)

            def form_x1b(t, dst=x1b):
                if dst is x1b:
                    need(pool, s["out"], t)
                pool.wait_ge(s["x1"], t + 1)
                pool.wait_ge(s["bb"], t + 1)
                g.tensor_tensor(dst[:, :], x1[:, :], base_bias[:, :], ALU.add).then_inc(s["x1b"], 1)

            def step(t, has):
                form_base_bias(t - 1)
                form_xb(t)
                form_x1b(t - 1)
                split_mix(t)
                split_x1(t)
                if has(2):
                    split_x(t + 2)

            g.memset(mix[:, :, :], 0.0).then_inc(mix_zero, 1)
            g.memset(ones[:, :], 1.0).then_inc(ones_ready, 1)
            split_x(1)
            pool.wait_ge(l_wa[1], 16)
            g.tensor_tensor(k_sums[:, :, 0:AR + DH], wa_raw[1][:, 0:2, :], wa_raw[1][:, 2:4, :],
                            ALU.add).then_inc(k_summed, 1)
            pool.wait_ge(l_wb[1], 16)
            g.tensor_tensor(k_sums[:, :, AR + DH:AR + D], wb_raw[1][:, 0:2, :], wb_raw[1][:, 2:4, :],
                            ALU.add).then_inc(k_summed, 1)
            pool.wait_ge(k_summed, 2)
            g.tensor_tensor(k_sum[:, :], k_sums[:, 0, :], k_sums[:, 1, :], ALU.add).then_inc(k_summed, 1)
            pool.wait_ge(l_bias[0], 16)
            form_xb(0)
            split_x1(0)
            split_mix(0)
            split_x(2)
            pool.wait_ge(l_bias[1], 16)
            stages(pool, step)
            form_base_bias(LAST - 1)
            form_xb(LAST)
            form_x1b(LAST - 1)
            split_mix(LAST)
            form_base_bias(LAST)
            form_x1b(LAST, dst=base_bias)


def kernel(**inputs):
    import numpy as np
    import concourse.bacc as bacc
    from concourse.bass_utils import run_bass_kernel_spmd as run

    i = {k: np.asarray(v) for k, v in inputs.items()}
    x = i["x"]
    lead = TAPS // 2
    xp = np.zeros((TILES, SPT, HALVES, CH, NBP, PH), x.dtype)
    xp.reshape(TILES, SPT, HALVES, CH, NBP * PH)[..., lead:lead + D] = x.reshape(TILES, SPT, HALVES, CH, D)
    xp = xp.transpose(0, 3, 5, 2, 1, 4)[..., PAIRS, :]
    w = i["L0_cond_weight"]
    cw = np.zeros((CH, PH, HALVES, SHIFTS, PH, CH), w.dtype)
    cg = C // GROUPS
    for sh in range(SHIFTS):
        for pi in range(PH):
            for po in range(PH):
                k = PH * sh + pi - po
                if 0 <= k < TAPS:
                    for g in range(GROUPS):
                        h, q = divmod(g * cg, CH)
                        cw[q:q + cg, pi, h, sh, po, q:q + cg] = w[g * cg:(g + 1) * cg, :, k].T
    wk = i["L1_cond_weight"][..., 0]
    kern = np.tile(wk.transpose(0, 2, 1).reshape(E, C * C), (SPT, 1))
    bk = np.zeros((SPT, E, SPT, C), wk.dtype)
    for j in range(SPT):
        bk[j, :, j, :] = i["L1_cond_bias_k"]

    def weights(layer, order):
        wb, a, r, b = (i[f"L{layer}_ffn_{n}"] for n in ("W_base", "A", "W_router", "B"))
        return {
            f"wa{layer}": order(np.concatenate([a.reshape(ER, D).T, r.T, wb.T[:, :DH]], axis=1)),
            f"wb{layer}": order(wb.T[:, DH:]),
            f"lb{layer}": b.transpose(0, 2, 1).reshape(ER, D),
            f"bias{layer}": np.tile(i[f"L{layer}_ffn_b_base"], (P, 1)),
        }

    f = np.float32
    halves = lambda a: np.concatenate([np.tile(a[..., h * CH:(h + 1) * CH], PH) for h in range(HALVES)], -1)
    pack = {
        "condT": i["cond_128"].T,
        "cw": halves(i["L0_cond_c_weight"].T),
        "W0": i["L1_cond_W0"], "W1": i["L1_cond_W1"], "W2": i["L1_cond_W2"],
        "side": halves(i["fside_S_0"]).reshape(HALVES, P).T,
        "b0": i["L1_cond_b0"][:, None], "b1": i["L1_cond_b1"][:, None],
        "b2": np.tile(i["L1_cond_b2"], (P, 1)),
        "ident": np.eye(P, dtype=f),
        "iota": np.tile(np.arange(E, dtype=f), (P, 1)),
        "own": np.repeat(np.tile(np.eye(SPT, dtype=f), (P // SPT, 1)), E, axis=1),
    }
    assert {k: a.shape[1] for k, a in pack.items()} == PACK
    arrays = {
        "x_phase": xp.reshape(TILES, P, HALVES, SPT, NBP),
        "x_tok": x.reshape(TILES, P, D),
        "conv_w": cw.reshape(P, HALVES, SHIFTS, P),
        **weights(0, lambda a: a.reshape(NB, 2, KT, -1).transpose(1, 0, 2, 3).reshape(P, KT, -1)),
        **weights(1, lambda a: a.reshape(KT, P, -1).transpose(1, 0, 2)),
        "pack": np.concatenate(list(pack.values()), axis=1),
        "kern": kern, "bk": bk.reshape(SPT * E, P),
    }
    arrays = {k: np.ascontiguousarray(a) for k, a in arrays.items()}
    nc = bacc.Bacc("TRN2", target_bir_lowering=False, num_devices=1)
    d = {k: nc.dram_tensor(f"in_{k}", a.shape, F32, kind="ExternalInput").ap() for k, a in arrays.items()}
    d["out"] = nc.dram_tensor("out", (TILES, P, D), F32, kind="ExternalOutput").ap()
    d["scratch"] = nc.dram_tensor("scratch", (N, C * C), F32, kind="Internal").ap()
    build(nc, d)
    r = run(nc, [{f"in_{k}": a for k, a in arrays.items()}], core_ids=[0])
    return r.results[0]["out"].reshape(N, C, D)
```
